# Optimizing a Trainium2 kernel written in Bass

```python
import numpy as np
import jax
import jax.numpy as jnp

def _softmax(x, axis=-1):
    return jax.nn.softmax(x, axis=axis)

def _gelu(x):
    return jax.nn.gelu(x, approximate=True)

def _silu(x):
    return jax.nn.silu(x)

def _sigmoid(x):
    return jax.nn.sigmoid(x)

def _layernorm(x, axis=-1, eps=1e-05):
    m = jnp.mean(x, axis=axis, keepdims=True)
    v = jnp.var(x, axis=axis, keepdims=True)
    return (x - m) / jnp.sqrt(v + eps)

def _scatter_add(tgt, idx, src, axis=0):
    return tgt.at[idx].add(src)

def _segment_sum(src, seg, n):
    return jax.ops.segment_sum(src, seg, n)
kernel_name = 'mk_decoder_postln_d1_seqx_r4_29e252'

def setup_inputs(seed: int=0):
    np.random.seed(seed)
    _w = jnp.asarray

    def _rec_inputs():
        import jax
        import jax.numpy as jnp
        _rk = jax.random.key(seed)
        x = 0.000341 + 1 * jax.random.normal(jax.random.fold_in(_rk, 1), (16, 256, 512), jnp.float32)
        _lenS = 256 - jax.random.randint(jax.random.fold_in(_rk, 7), (16,), 0, max(1, 256 // 4) + 1, jnp.int32)
        _lenS2 = 256 - jax.random.randint(jax.random.fold_in(_rk, 8), (16,), 0, max(1, 256 // 4) + 1, jnp.int32)
        _ctx_2048P = jax.random.normal(jax.random.fold_in(_rk, 11), (16, 16, 512), jnp.float32)
        _ctx_2048c = jax.random.dirichlet(jax.random.fold_in(_rk, 511), 0.3 * jnp.ones((16,), jnp.float32), (16, 256))
        _ctx_2048t = jnp.einsum('bsk,bkd->bsd', _ctx_2048c, _ctx_2048P)
        _ctx_2048t = _ctx_2048t * jax.lax.rsqrt(jnp.mean(jnp.square(_ctx_2048t)) + 1e-12) * 0.953939
        ctx_2048 = -1.47943e-05 + 1.00017 * (_ctx_2048t + 0.3 * jax.random.normal(jax.random.fold_in(_rk, 611), (16, 256, 512), jnp.float32))
        return (x, ctx_2048)
    x, ctx_2048 = _rec_inputs()

    def _L0_attn_setup():
        import jax, jax.numpy as jnp
        import numpy as np
        N_HEAD = 16
        key = jax.random.key(seed)
        ks = jax.random.split(key, 9)
        H = 512

        def w(k, shape, scale=0.02):
            return jax.random.normal(k, shape, dtype=jnp.float32) * scale
        return {'h': jax.random.normal(ks[0], (4, 512, H), dtype=jnp.float32), 'Wq': w(ks[1], (H, H)), 'bq': w(ks[2], (H,)), 'Wk': w(ks[3], (H, H)), 'bk': w(ks[4], (H,)), 'Wv': w(ks[5], (H, H)), 'bv': w(ks[6], (H,)), 'Wo': w(ks[7], (H, H)), 'bo': w(ks[8], (H,))}
    _L0_attn_all = _L0_attn_setup()
    _L0_attn_in = {k: v for k, v in _L0_attn_all.items() if k in ('Wq', 'bq', 'Wk', 'bk', 'Wv', 'bv', 'Wo', 'bo')}
    del _L0_attn_all

    def _L0_xattn_setup():
        import jax, jax.numpy as jnp
        import numpy as np

        def _wkv(time_decay, time_first, k, v):
            w = -jnp.exp(time_decay)
            u = time_first
            B, T, C = k.shape
            aa = jnp.zeros((B, C), dtype=k.dtype)
            bb = jnp.zeros((B, C), dtype=k.dtype)
            pp = jnp.full((B, C), -1e+38, dtype=k.dtype)

            def step(carry, kv_t):
                aa, bb, pp = carry
                kt, vt = kv_t
                ww = u + kt
                q = jnp.maximum(pp, ww)
                e1 = jnp.exp(pp - q)
                e2 = jnp.exp(ww - q)
                y_t = (e1 * aa + e2 * vt) / (e1 * bb + e2)
                ww2 = pp + w
                q2 = jnp.maximum(ww2, kt)
                e1b = jnp.exp(ww2 - q2)
                e2b = jnp.exp(kt - q2)
                new_carry = (e1b * aa + e2b * vt, e1b * bb + e2b, q2)
                return (new_carry, y_t)
            ks = jnp.transpose(k, (1, 0, 2))
            vs = jnp.transpose(v, (1, 0, 2))
            _, ys = jax.lax.scan(step, (aa, bb, pp), (ks, vs))
            return jnp.transpose(ys, (1, 0, 2))
        key = jax.random.key(seed)
        k1, k2, k3, k4 = jax.random.split(key, 4)
        B, T, C = (8, 256, 512)
        return {'batch_size': B, 'seq_len': T, 'embedding_dim': C, 'time_decay': jax.random.normal(k1, (C,), dtype=jnp.float32), 'time_first': jax.random.normal(k2, (C,), dtype=jnp.float32), 'k': jax.random.normal(k3, (B, T, C), dtype=jnp.float32), 'v': jax.random.normal(k4, (B, T, C), dtype=jnp.float32)}
    _L0_xattn_all = _L0_xattn_setup()
    _L0_xattn_in = {k: v for k, v in _L0_xattn_all.items() if k in ('time_decay', 'time_first')}
    del _L0_xattn_all

    def _L0_ffn_setup():
        import jax, jax.numpy as jnp
        import numpy as np
        import math
        N_EMBD = 512
        N_HEAD = 16
        HEAD_DIM = N_EMBD // N_HEAD
        B, T = (2, 512)
        key = jax.random.key(seed)
        k1, k2, k3 = jax.random.split(key, 3)
        x = jax.random.normal(k1, (B, T, N_EMBD), dtype=jnp.float32)
        W_gate = jax.random.normal(k2, (N_HEAD, N_EMBD), dtype=jnp.float32) * 0.02
        W_qkv = jax.random.normal(k3, (3 * N_EMBD, N_EMBD), dtype=jnp.float32) * 0.02
        return {'x': x, 'W_gate': W_gate, 'W_qkv': W_qkv}
    _L0_ffn_all = _L0_ffn_setup()
    _L0_ffn_in = {k: v for k, v in _L0_ffn_all.items() if k in ('W_gate', 'W_qkv')}
    del _L0_ffn_all
    return {'x': x, 'ctx_2048': ctx_2048, 'L0_attn_Wq': _L0_attn_in['Wq'], 'L0_attn_bq': _L0_attn_in['bq'], 'L0_attn_Wk': _L0_attn_in['Wk'], 'L0_attn_bk': _L0_attn_in['bk'], 'L0_attn_Wv': _L0_attn_in['Wv'], 'L0_attn_bv': _L0_attn_in['bv'], 'L0_attn_Wo': _L0_attn_in['Wo'], 'L0_attn_bo': _L0_attn_in['bo'], 'L0_xattn_time_decay': _L0_xattn_in['time_decay'], 'L0_xattn_time_first': _L0_xattn_in['time_first'], 'L0_ffn_W_gate': _L0_ffn_in['W_gate'], 'L0_ffn_W_qkv': _L0_ffn_in['W_qkv']}

def reference(x, ctx_2048, L0_attn_Wq, L0_attn_bq, L0_attn_Wk, L0_attn_bk, L0_attn_Wv, L0_attn_bv, L0_attn_Wo, L0_attn_bo, L0_xattn_time_decay, L0_xattn_time_first, L0_ffn_W_gate, L0_ffn_W_qkv):
    import jax
    import jax.numpy as jnp

    def _L0_attn_ref(h, Wq, bq, Wk, bk, Wv, bv, Wo, bo):
        import jax, jax.numpy as jnp
        import numpy as np
        N_HEAD = 16
        B, S, H = h.shape
        nh = N_HEAD
        hd = H // nh
        q = (h @ Wq.T + bq).reshape(B, S, nh, hd)
        k = (h @ Wk.T + bk).reshape(B, S, nh, hd)
        v = (h @ Wv.T + bv).reshape(B, S, nh, hd)
        scale = 1.0 / jnp.sqrt(jnp.float32(hd))
        scores = jnp.einsum('bqhd,bkhd->bhqk', q, k) * scale
        causal = jnp.tril(jnp.ones((S, S), dtype=bool))
        scores = jnp.where(causal, scores, jnp.finfo(scores.dtype).min)
        attn = jax.nn.softmax(scores, axis=-1)
        o = jnp.einsum('bhqk,bkhd->bqhd', attn, v).reshape(B, S, H)
        return o @ Wo.T + bo

    def _L0_xattn_ref(batch_size, seq_len, embedding_dim, time_decay, time_first, k, v):
        import jax, jax.numpy as jnp
        import numpy as np

        def _wkv(time_decay, time_first, k, v):
            w = -jnp.exp(time_decay)
            u = time_first
            B, T, C = k.shape
            aa = jnp.zeros((B, C), dtype=k.dtype)
            bb = jnp.zeros((B, C), dtype=k.dtype)
            pp = jnp.full((B, C), -1e+38, dtype=k.dtype)

            def step(carry, kv_t):
                aa, bb, pp = carry
                kt, vt = kv_t
                ww = u + kt
                q = jnp.maximum(pp, ww)
                e1 = jnp.exp(pp - q)
                e2 = jnp.exp(ww - q)
                y_t = (e1 * aa + e2 * vt) / (e1 * bb + e2)
                ww2 = pp + w
                q2 = jnp.maximum(ww2, kt)
                e1b = jnp.exp(ww2 - q2)
                e2b = jnp.exp(kt - q2)
                new_carry = (e1b * aa + e2b * vt, e1b * bb + e2b, q2)
                return (new_carry, y_t)
            ks = jnp.transpose(k, (1, 0, 2))
            vs = jnp.transpose(v, (1, 0, 2))
            _, ys = jax.lax.scan(step, (aa, bb, pp), (ks, vs))
            return jnp.transpose(ys, (1, 0, 2))
        assert seq_len <= 256
        return _wkv(time_decay, time_first, k, v)

    def _L0_ffn_ref(x, W_gate, W_qkv):
        import jax, jax.numpy as jnp
        import numpy as np
        import math
        N_EMBD = 512
        N_HEAD = 16
        HEAD_DIM = N_EMBD // N_HEAD
        B, T = (2, 512)
        Bb, Tt, C = x.shape
        H, hd = (N_HEAD, HEAD_DIM)
        gating = jax.nn.softmax(x @ W_gate.T, axis=-1)
        idx = jnp.argmax(gating, axis=-1)
        indicator = jax.nn.one_hot(idx, H, dtype=gating.dtype)
        top1_val = jnp.max(gating, axis=-1, keepdims=True)
        gating_top1 = indicator * top1_val
        qkv = x @ W_qkv.T
        q, k, v = jnp.split(qkv, 3, axis=-1)
        k = k.reshape(Bb, Tt, H, hd)
        v = v.reshape(Bb, Tt, H, hd)
        k_shared = jnp.einsum('bth,bthd->btd', indicator, k)
        v_shared = jnp.einsum('bth,bthd->btd', gating_top1, v)
        q = q.reshape(Bb, Tt, H, hd).transpose(0, 2, 1, 3)
        att = jnp.einsum('bhqd,bkd->bhqk', q, k_shared) * (1.0 / math.sqrt(hd))
        causal = jnp.tril(jnp.ones((Tt, Tt), dtype=bool))
        att = jnp.where(causal[None, None, :, :], att, -jnp.inf)
        att = jax.nn.softmax(att, axis=-1)
        y = jnp.einsum('bhqk,bkd->bhqd', att, v_shared)
        y = y.transpose(0, 2, 1, 3).reshape(Bb, Tt, C)
        return y
    x = _layernorm(x + _L0_attn_ref(x, L0_attn_Wq, L0_attn_bq, L0_attn_Wk, L0_attn_bk, L0_attn_Wv, L0_attn_bv, L0_attn_Wo, L0_attn_bo), axis=-1)
    x = _layernorm(x + _L0_xattn_ref(16, 256, 512, L0_xattn_time_decay, L0_xattn_time_first, x, ctx_2048), axis=-1)
    x = _layernorm(x + _L0_ffn_ref(x, L0_ffn_W_gate, L0_ffn_W_qkv), axis=-1)
    return x

_drawn_inputs = setup_inputs


def setup_inputs(seed=0):
    import zlib

    import numpy as np

    out = dict(_drawn_inputs(seed))
    spreads = {}
    factors = {'L0_attn_Wq': 8.0,
     'L0_attn_bq': 8.0,
     'L0_attn_Wk': 8.0,
     'L0_attn_bk': 8.0,
     'L0_attn_bv': 7.577,
     'L0_attn_bo': 3.695,
     'L0_ffn_W_gate': 3.974,
     'L0_ffn_W_qkv': 2.949}
    for name, (base, spread) in spreads.items():
        noise = np.random.default_rng([zlib.crc32(name.encode()), seed]).standard_normal(out[name].shape)
        drawn = base * np.exp(spread * noise) if base else spread * noise
        out[name] = jnp.asarray(drawn.astype(out[name].dtype))
    for name, factor in factors.items():
        out[name] = (out[name] * factor).astype(out[name].dtype)
    return out
```

```python
import concourse.bass as bass
from concourse import mybir
from contextlib import ExitStack

NB, S, D = 16, 256, 512
NH, HD = 16, 32
P = 128
CC = D // P
TT = S // P
NG = 4
HG = NH // NG
SCALE = float(HD) ** -0.5
EPS = 1e-5
MASKED = -1e30
START_MAX = -1e38

W_Q, W_K, W_V, W_O, W_FQ, W_FK, W_FV = range(7)
NW = 7

A_JOBS, A_QJ, A_KJ, A_VJ, A_MJ, A_OTJ, A_WOJ = 16, 0, 2, 4, 6, 10, 14
F_JOBS, F_QJ, F_GATEJ, F_KJ, F_VJ, F_KTJ, F_MJ = 12, 0, 2, 3, 5, 7, 8
TILES = 3 * NG
W_JOBS, W_X1J, W_YJ, W_X2J = 6, 0, 2, 4
CONSTS = 2


def build(nc, x_d, xT_d, ctxT_d, weights_d, gate_d, ch_bias_d, row_bias_d, decay_d, first_d, out_d):
    f32, f32r, bf16 = mybir.dt.float32, mybir.dt.float32r, mybir.dt.bfloat16
    ALU, ACT, AX = mybir.AluOpType, mybir.ActivationFunctionType, mybir.AxisListType
    V, A, T, G = nc.vector, nc.scalar, nc.tensor, nc.gpsimd

    ctx = ExitStack()
    with ctx:
        def sb(name, shape, dt=f32):
            return ctx.enter_context(nc.sbuf_tensor(name, shape, dt))

        def overlaid(name, size, *tensors):
            base = nc.sbuf_base
            sb(name, [P, size // 4])
            return [nc.alloc_sbuf_tensor_at(n, shape, dt, offset=base + at) for n, shape, dt, at in tensors]

        def pb(name):
            return ctx.enter_context(nc.psum_tensor(name, [P, 512], f32))

        def sem(name):
            return ctx.enter_context(nc.semaphore(name))

        w_hi = sb("w_hi", [P, NW, CC, D], f32r)
        w_lo = sb("w_lo", [P, NW, CC, D], f32r)
        gate_hi = sb("gate_hi", [P, CC, NH], f32r)
        gate_lo = sb("gate_lo", [P, CC, NH], f32r)
        gate_raw = sb("gate_raw", [P, CC, NH])
        q_stack = sb("q_stack", [P, NH, S], f32r)
        k_stack = sb("k_stack", [P, NH, S], f32r)
        kf_stack = sb("kf_stack", [P, S], f32r)
        q_hi, x_raw = overlaid("q_region", CC * S * 4,
                               ("q_hi", [P, CC, S], f32r, 0),
                               ("x_raw", [P, CC, S], f32, 0))
        q_lo = sb("q_lo", [P, CC, S], f32r)
        HC = CC // 2
        half = HC * S * 4
        k_hi, k_lo, w_key, w_e1, w_d, w_ev = overlaid(
            "k_region", 4 * half,
            ("k_hi", [P, CC, S], f32r, 0), ("k_lo", [P, CC, S], f32r, 2 * half),
            ("w_key", [P, HC, S], f32, 0), ("w_e1", [P, HC, S], f32, half),
            ("w_d", [P, HC, S], f32, 2 * half), ("w_ev", [P, HC, S], f32, 3 * half))
        xt_hi = sb("xt_hi", [P, CC, S], f32r)
        xt_lo = sb("xt_lo", [P, CC, S], f32r)
        xa = sb("xa", [P, TT, D])
        xb = sb("xb", [P, TT, D])
        v_a = sb("v_a", [P, TT, NH, HD + 1])
        v_f = sb("v_f", [P, TT, HD + 1])
        prob0 = sb("prob0", [P, HG, S])
        prob1 = sb("prob1", [P, HG, P])
        picked = prob0[:].rearrange("p h q -> p (h q)")[:, 0:D].rearrange("p (h d) -> p h d", h=NH)
        o_tok = sb("o_tok", [P, TT, HG * HD])
        bo_row = sb("bo_row", [P, D])
        ch_bias = sb("ch_bias", [P, 3, CC])
        neg_max = sb("neg_max", [P, 2, TT * HG])
        max_hi = sb("max_hi", [TT * HG, P], f32r)
        max_lo = sb("max_lo", [TT * HG, P], f32r)
        ident = sb("ident", [P, P])
        ident_b = sb("ident_b", [P, P], bf16)
        mask_qk = sb("mask_qk", [P, P], bf16)
        mask_kq = sb("mask_kq", [P, P], bf16)
        o_rec = sb("o_rec", [P, TT * HG])
        w_val = sb("w_val", [P, HC, S])
        w_max = sb("w_max", [P, HC, S + 1])
        w_e2 = sb("w_e2", [P, HC, S + 1])
        w_y = sb("w_y", [P, 2, HC, S])
        decay = sb("decay", [P, CC])
        first = sb("first", [P, CC])
        stats = sb("stats", [P, 3, TT, 6])
        spare = sb("spare", [P, 1])
        eps = sb("eps", [P, TT])
        meanvar = sb("meanvar", [P, 3, TT, 2])
        var_eps = sb("var_eps", [P, 3, TT])
        rstd = sb("rstd", [P, 3, TT])
        minus_half = sb("minus_half", [P, TT])
        logit = sb("logit", [P, TT, NH])
        g_max = sb("g_max", [P, TT])
        g_nmax = sb("g_nmax", [P, TT])
        g_eq = sb("g_eq", [P, TT, NH])
        g_rank = sb("g_rank", [P, TT, NH])
        g_top = sb("g_top", [P, TT])
        g_ind = sb("g_ind", [P, TT, NH])
        g_exp = sb("g_exp", [P, TT, NH])
        g_sum = sb("g_sum", [P, TT])
        g_val = sb("g_val", [P, TT])
        rank = sb("rank", [P, NH])
        k_sel = sb("k_sel", [P, TT, HD])
        v_sel = sb("v_sel", [P, TT, HD])
        k3 = sb("k3", [P, TT, 3, HD], f32r)

        gen = [pb("gen0"), pb("gen1")]
        sq = [pb("sq0"), pb("sq1")]
        sk = [pb("sk0"), pb("sk1")]
        po = pb("po")
        pw = pb("pw")

        load_w = [sem(f"load_w{i}") for i in range(4)]
        load_c = sem("load_c")
        load_xr, load_xa, load_v = sem("load_xr"), sem("load_xa"), sem("load_v")
        w_split_hi, w_split_lo = sem("w_split_hi"), sem("w_split_lo")
        consts, zero_done = sem("consts"), sem("zero_done")
        xt_hi_ready, xt_ready, xa_ready = sem("xt_hi_ready"), sem("xt_ready"), sem("xa_ready")
        a_job, a_free, f_job, f_free = sem("a_job"), sem("a_free"), sem("f_job"), sem("f_free")
        a_sq, a_max, f_sq, f_max = sem("a_sq"), sem("a_max"), sem("f_sq"), sem("f_max")
        a_sk, a_exp, f_sk, f_exp = sem("a_sk"), sem("a_exp"), sem("f_sk"), sem("f_exp")
        a_po, a_norm, f_po, f_norm = sem("a_po"), sem("a_norm"), sem("f_po"), sem("f_norm")
        a_hi, f_hi = sem("a_hi"), sem("f_hi")
        a_stk = [sem(f"a_stk{g}") for g in range(NG)]
        f_stk = [sem(f"f_stk{g}") for g in range(NG)]
        a_mrow = [sem(f"a_mrow{g}") for g in range(NG)]
        f_mrow = [sem(f"f_mrow{g}") for g in range(NG)]
        w_job, w_free, x2_hi = sem("w_job"), sem("w_free"), sem("x2_hi")
        w_pp, w_diff, w_carry, w_min = sem("w_pp"), sem("w_diff"), sem("w_carry"), sem("w_min")
        w_evr, w_scan, w_now, w_den = sem("w_evr"), sem("w_scan"), sem("w_now"), sem("w_den")
        w_rec, w_yr = sem("w_rec"), sem("w_yr")
        ln_stat = [sem(f"ln_stat{n}") for n in range(3)]
        ln_rstd = [sem(f"ln_rstd{n}") for n in range(3)]
        x1_ready, x2_ready, x3_ready = sem("x1_ready"), sem("x2_ready"), sem("x3_ready")
        g_ready, g_summed = sem("g_ready"), sem("g_summed")
        stored = sem("stored")
        dve_a, dve_w, dve_f, dve_0 = sem("dve_a"), sem("dve_w"), sem("dve_f"), sem("dve_0")
        pool_w, pool_0 = sem("pool_w"), sem("pool_0")
        pool_ln = [sem(f"pool_ln{n}") for n in range(3)]
        act_0 = sem("act_0")

        def slot(n):
            if n % 4 < 2:
                return prob0[:].rearrange("p h q -> p (h q)")[:, D * (n % 2):D * (n % 2 + 1)]
            return xb[:, n % 2, :]

        def wait(eng, s, value):
            if not isinstance(value, int) or value > 0:
                eng.wait_ge(s, value)

        class Chain:
            def __init__(self, eng, s, per, b):
                self.eng, self.s, self.base, self.per, self.n = eng, s, per * b, per, 0

            def mark(self, ins):
                ins.then_inc(self.s, 1)
                self.n += 1

            def wait(self):
                self.eng.wait_ge(self.s, self.base + self.n)

            def link(self, ins):
                self.mark(ins)
                self.wait()

            def close(self):
                assert self.n == self.per, self.n

        def last(b):
            return min(b + 2, NB) if isinstance(b, int) else b + 2

        DVE_F_K3 = 12
        block = ctx.enter_context(nc.Block())

        @block.sync
        def _(sp):
            def load_xr_of(b, stk, count):
                for g in range(NG):
                    wait(sp, stk[g], count)
                sp.dma_start(x_raw[:], xT_d[b].rearrange("(c p) t -> p c t", p=P)).then_inc(load_xr, 16)

            def stack(dst, lo, src, g, s):
                sp.dma_start(dst[lo:lo + HD, HG * g:HG * (g + 1), :].bitcast(f32),
                             src[HD * g:HD * (g + 1), :, :].bitcast(f32)).then_inc(s, 16)

            def max_rows(b, g, free, job, per, s):
                wait(sp, free, per * b + job + g + 1)
                for row, src in ((3 * HD, max_hi), (3 * HD + 1, max_lo)):
                    for c in range(TT):
                        sp.dma_start(q_stack[row:row + 1, HG * g:HG * (g + 1), P * c:P * (c + 1)].bitcast(f32),
                                     src[HG * c:HG * (c + 1), :].bitcast(f32)).then_inc(s[g], 16)

            def load_ctx(b, half):
                wait(sp, w_yr, 2 * b + half)
                rows = slice(HC * P * half, HC * P * (half + 1))
                sp.dma_start(w_val[:], ctxT_d[b, rows].rearrange("(c p) t -> p c t", p=P)).then_inc(load_v, 16)

            def store(b):
                wait(sp, x3_ready, b + 1)
                sp.dma_start(out_d[b].rearrange("(c p) d -> p c d", p=P), xb[:]).then_inc(stored, 16)

            def iteration(t, do_a, do_f, prefetch, do_store):
                if do_a:
                    wait(sp, a_free, A_JOBS * t + A_QJ + 2)
                    for g in range(NG):
                        for lo, src in ((0, q_hi), (HD, q_hi), (2 * HD, q_lo)):
                            stack(q_stack, lo, src, g, a_stk[g])
                    wait(sp, a_free, A_JOBS * t + A_KJ + 2)
                    for g in range(NG):
                        for lo, src in ((0, k_hi), (HD, k_lo), (2 * HD, k_hi)):
                            stack(k_stack, lo, src, g, a_stk[g])
                if do_store:
                    store(t - 2)
                if do_a:
                    wait(sp, w_free, W_JOBS * (t - 1) + W_YJ + 2)
                    sp.dma_start(xa[:], x_d[t].rearrange("(c p) d -> p c d", p=P)).then_inc(load_xa, 16)
                    load_ctx(t, 0)
                    for g in range(NG):
                        max_rows(t, g, a_free, A_MJ, A_JOBS, a_mrow)
                if prefetch and not do_f:
                    load_xr_of(t + 1, a_stk, 96 * (t + 1))
                if do_f:
                    b = t - 1
                    wait(sp, f_free, F_JOBS * b + F_QJ + 2)
                    for g in range(NG):
                        for lo, src in ((0, q_hi), (HD, q_hi), (2 * HD, q_lo)):
                            stack(q_stack, lo, src, g, f_stk[g])
                    if prefetch:
                        load_xr_of(t + 1, f_stk, 48 * t)
                    for g in range(NG):
                        max_rows(b, g, f_free, F_MJ, F_JOBS, f_mrow)
                        if g == 2 and do_a:
                            load_ctx(t, 1)
                elif do_a:
                    load_ctx(t, 1)

            sp.dma_start(ch_bias[:], ch_bias_d).then_inc(load_c, 16)
            sp.dma_start(decay[:], decay_d).then_inc(load_c, 16)
            sp.dma_start(first[:], first_d).then_inc(load_c, 16)
            sp.dma_start(bo_row[:], row_bias_d).then_inc(load_c, 16)
            sp.dma_start(gate_raw[:], gate_d.rearrange("(c p) h -> p c h", p=P)).then_inc(load_c, 16)
            load_xr_of(0, a_stk, 0)
            for n in range(NW * CC):
                wait(sp, w_split_lo, n - 3)
                sp.dma_start(slot(n), weights_d[n // CC, n % CC]).then_inc(load_w[n % 4], 16)
            iteration(0, True, False, True, False)
            iteration(1, True, True, True, False)
            with sp.Fori(2, NB - 1) as t:
                iteration(t, True, True, True, True)
            iteration(NB - 1, True, True, False, True)
            iteration(NB, False, True, False, True)
            store(NB - 1)
            sp.wait_ge(stored, 16 * NB)

        @block.tensor
        def _(pe):
            def products(out, lhs, rhs):
                for c in range(CC):
                    (lh, ll), (rh, rl) = lhs(c), rhs(c)
                    T.matmul(out, lh, rh, start=(c == 0), stop=False, skip_group_check=True)
                    T.matmul(out, lh, rl, start=False, stop=False, skip_group_check=True)
                    mm = T.matmul(out, ll, rh, start=False, stop=(c == CC - 1), skip_group_check=True)
                return mm

            def weight(w, lo, n):
                return lambda c: (w_hi[:, w, c, lo:lo + n], w_lo[:, w, c, lo:lo + n])

            def tokens(lo, n, hi_t=xt_hi, lo_t=xt_lo):
                return lambda c: (hi_t[:, c, lo:lo + n], lo_t[:, c, lo:lo + n])

            def channels_out(n, w, pair):
                for i in range(2):
                    mm = products(gen[n % 2][:, S * i:S * (i + 1)], weight(w, P * (2 * pair + i), P), tokens(0, S))
                return mm

            def tokens_out(n, w, c, hi_t=xt_hi, lo_t=xt_lo):
                return products(gen[n % 2][:, 0:D], tokens(P * c, P, hi_t, lo_t), weight(w, 0, D))

            def scores_sq(b, g, stk, per, key, s_sq, s_max):
                pe.wait_ge(stk[g], per * (b + 1))
                for i in range(3):
                    n = 3 * g + i
                    if n >= 2:
                        pe.wait_ge(s_max, TILES * b + n - 1)
                    out = sq[n % 2]
                    if i == 0:
                        for k in range(HG):
                            h = HG * g + k
                            T.matmul(out[:, P * k:P * (k + 1)], q_stack[0:3 * HD, h, 0:P], key(h, 0, P, 3 * HD),
                                     start=(k == 0), stop=False, skip_group_check=True)
                        mm = None
                        for k in range(HG):
                            mm = T.matmul(out[:, P * k:P * (k + 1)], ident_b[:], mask_qk[:],
                                          start=False, stop=(k == HG - 1), skip_group_check=True)
                    else:
                        for k in range(2):
                            h = HG * g + 2 * (i - 1) + k
                            T.matmul(out[:, S * k:S * (k + 1)], q_stack[0:3 * HD, h, P:S], key(h, 0, S, 3 * HD),
                                     start=(k == 0), stop=False, skip_group_check=True)
                        for k in range(2):
                            mm = T.matmul(out[:, S * k + P:S * (k + 1)], ident_b[:], mask_qk[:],
                                          start=False, stop=(k == 1), skip_group_check=True)
                    mm.then_inc(s_sq, 1)

            def max_transpose(b, g, job, jobs, s_job, s_free, s_max):
                n = job + g
                pe.wait_ge(s_max, TILES * b + 3 * (g + 1))
                pe.wait_ge(s_free, jobs * b + n - 1)
                T.transpose(gen[n % 2][0:TT * HG, 0:P], neg_max[:, g % 2, :], ident[:]).then_inc(s_job, 1)

            def scores_sk(b, g, mrow, key, s_sk, s_exp):
                pe.wait_ge(mrow[g], 64 * (b + 1))
                rows = 3 * HD + 2
                for i in range(3):
                    n = 3 * g + i
                    if n >= 2:
                        pe.wait_ge(s_exp, TILES * b + n - 1)
                    out = sk[n % 2]
                    if i < 2:
                        for k in range(2):
                            h = HG * g + 2 * i + k
                            T.matmul(out[:, S * k:S * (k + 1)], key(h, 0, P, rows), q_stack[0:rows, h, :],
                                     start=(k == 0), stop=False, skip_group_check=True)
                        for k in range(2):
                            mm = T.matmul(out[:, S * k:S * k + P], ident_b[:], mask_kq[:],
                                          start=False, stop=(k == 1), skip_group_check=True)
                    else:
                        for k in range(HG):
                            h = HG * g + k
                            T.matmul(out[:, P * k:P * (k + 1)], key(h, P, P, rows), q_stack[0:rows, h, P:S],
                                     start=(k == 0), stop=False, skip_group_check=True)
                        for k in range(HG):
                            mm = T.matmul(out[:, P * k:P * (k + 1)], ident_b[:], mask_kq[:],
                                          start=False, stop=(k == HG - 1), skip_group_check=True)
                    mm.then_inc(s_sk, 1)

            def values(b, g, value, s_exp, s_norm, s_po):
                if g:
                    pe.wait_ge(s_norm, NG * b + g)
                pe.wait_ge(s_exp, TILES * b + 3 * (g + 1))
                out = po[:, 0:TT * HG * (HD + 1)].rearrange("p (c h d) -> p c h d", c=TT, h=HG)
                for k in range(HG):
                    h = HG * g + k
                    T.matmul(out[:, 0, k, :], prob0[:, k, 0:P], value(0, h),
                             start=True, stop=True, skip_group_check=True)
                    T.matmul(out[:, 1, k, :], prob0[:, k, P:S], value(0, h),
                             start=True, stop=False, skip_group_check=True)
                    mm = T.matmul(out[:, 1, k, :], prob1[:, k, :], value(1, h),
                                  start=False, stop=True, skip_group_check=True)
                mm.then_inc(s_po, 1)

            def out_transpose(b, g):
                n = A_OTJ + g
                pe.wait_ge(a_norm, NG * b + g + 1)
                pe.wait_ge(a_free, A_JOBS * b + n - 1)
                for c in range(TT):
                    mm = T.transpose(gen[n % 2][:, P * c:P * (c + 1)], o_tok[:, c, :], ident[:])
                mm.then_inc(a_job, 1)

            def x_transpose(b, job, src, ready, count):
                for half in range(2):
                    n = job + half
                    pe.wait_ge(ready, count)
                    wait(pe, w_free, W_JOBS * b + n)
                    for i in range(HC):
                        for c in range(TT):
                            ch = P * (HC * half + i)
                            mm = T.transpose(pw[:, S * i + P * c:S * i + P * (c + 1)], src[:, c, ch:ch + P], ident[:])
                    mm.then_inc(w_job, 1)

            def y_transpose(b):
                for half in range(2):
                    pe.wait_ge(w_yr, 2 * b + half + 1)
                    pe.wait_ge(w_free, W_JOBS * b + W_YJ + half)
                    for c in range(TT):
                        for i in range(HC):
                            at = HC * P * c + P * i
                            mm = T.transpose(pw[:, at:at + P], w_y[:, half, i, P * c:P * (c + 1)], ident[:])
                    mm.then_inc(w_job, 1)

            def key_a(h, lo, n, rows):
                return k_stack[0:rows, h, lo:lo + n]

            def key_f(h, lo, n, rows):
                return kf_stack[0:rows, lo:lo + n]

            def stage_a(b, w2):
                pe.wait_ge(xt_ready, b + 1)
                wait(pe, f_free, F_JOBS * (b - 1))
                wait(pe, a_free, A_JOBS * b)
                for n in range(2):
                    channels_out(A_QJ + n, W_Q, n).then_inc(a_job, 1)
                for n in range(2):
                    pe.wait_ge(a_free, A_JOBS * b + A_KJ + n - 1)
                    channels_out(A_KJ + n, W_K, n).then_inc(a_job, 1)
                for c in range(TT):
                    pe.wait_ge(a_free, A_JOBS * b + A_VJ + c - 1)
                    tokens_out(A_VJ + c, W_V, c).then_inc(a_job, 1)
                if w2:
                    y_transpose(b - 1)
                wait(pe, f_max, TILES * (b - 1))
                wait(pe, a_max, TILES * b)
                wait(pe, f_exp, TILES * (b - 1))
                wait(pe, a_exp, TILES * b)
                wait(pe, f_norm, NG * (b - 1))
                wait(pe, a_norm, NG * b)
                for i in range(NG + 4):
                    if i < NG:
                        scores_sq(b, i, a_stk, 96, key_a, a_sq, a_max)
                    if 1 <= i <= NG:
                        max_transpose(b, i - 1, A_MJ, A_JOBS, a_job, a_free, a_max)
                    if i >= 4:
                        out_transpose(b, i - 4)
                    if 3 <= i < NG + 3:
                        if i == 3:
                            pe.wait_ge(a_free, A_JOBS * b + A_VJ + 2)
                        values(b, i - 3, lambda c, h: v_a[:, c, h, :], a_exp, a_norm, a_po)
                    if 2 <= i < NG + 2:
                        scores_sk(b, i - 2, a_mrow, key_a, a_sk, a_exp)
                    if i == 4 and w2:
                        x_transpose(b - 1, W_X2J, xb, x2_ready, b)
                for c in range(TT):
                    pe.wait_ge(a_free, A_JOBS * b + A_OTJ + NG)
                    tokens_out(A_WOJ + c, W_O, c, k_hi, k_lo).then_inc(a_job, 1)

            def stage_f(b, w1):
                pe.wait_ge(w_free, W_JOBS * (b + 1))
                for n in range(2):
                    pe.wait_ge(a_free, A_JOBS * last(b) - 1 + n)
                    channels_out(F_QJ + n, W_FQ, n).then_inc(f_job, 1)
                n = F_GATEJ
                pe.wait_ge(f_free, F_JOBS * b + n - 1)
                for c in range(TT):
                    mm = products(gen[n % 2][:, NH * c:NH * (c + 1)], tokens(P * c, P),
                                  lambda k: (gate_hi[:, k, :], gate_lo[:, k, :]))
                mm.then_inc(f_job, 1)
                for job, w in ((F_KJ, W_FK), (F_VJ, W_FV)):
                    for c in range(TT):
                        pe.wait_ge(f_free, F_JOBS * b + job + c - 1)
                        tokens_out(job + c, w, c).then_inc(f_job, 1)
                n = F_KTJ
                pe.wait_ge(f_free, F_JOBS * b + F_KJ + 2)
                pe.wait_ge(dve_f, 29 * b + DVE_F_K3)
                pe.wait_ge(f_free, F_JOBS * b + n - 1)
                for c in range(TT):
                    mm = T.transpose(gen[n % 2][0:3 * HD, P * c:P * (c + 1)],
                                     k3[:, c, :, :].rearrange("p a d -> p (a d)").bitcast(f32), ident[:])
                mm.then_inc(f_job, 1)
                if w1:
                    x_transpose(b + 1, W_X1J, xa, x1_ready, b + 2)
                wait(pe, a_max, TILES * last(b))
                wait(pe, a_exp, TILES * last(b))
                wait(pe, a_norm, NG * last(b))
                pe.wait_ge(f_free, F_JOBS * b + F_KTJ + 1)
                for i in range(NG + 3):
                    if i < NG:
                        scores_sq(b, i, f_stk, 48, key_f, f_sq, f_max)
                    if 1 <= i <= NG:
                        max_transpose(b, i - 1, F_MJ, F_JOBS, f_job, f_free, f_max)
                    if i >= 3:
                        values(b, i - 3, lambda c, h: v_f[:, c, :], f_exp, f_norm, f_po)
                    if 2 <= i < NG + 2:
                        scores_sk(b, i - 2, f_mrow, key_f, f_sk, f_exp)

            pe.wait_ge(consts, CONSTS)
            pe.wait_ge(w_split_lo, NW * CC + 1)
            stage_a(0, False)
            x_transpose(0, W_X1J, xa, x1_ready, 1)
            stage_a(1, True)
            stage_f(0, True)
            with pe.Fori(2, NB) as t:
                stage_a(t, True)
                stage_f(t - 1, True)
            y_transpose(NB - 1)
            x_transpose(NB - 1, W_X2J, xb, x2_ready, NB)
            stage_f(NB - 1, False)

        @block.scalar
        def _(act):
            def exps(b, g, s_sk, s_exp):
                for i in range(3):
                    n = 3 * g + i
                    act.wait_ge(s_sk, TILES * b + n + 1)
                    if i < 2:
                        dst = prob0[:, 2 * i:2 * i + 2, :].rearrange("p h q -> p (h q)")
                    else:
                        dst = prob1[:].rearrange("p h q -> p (h q)")
                    A.activation(dst, sk[n % 2][:], ACT.Exp, scale=SCALE).then_inc(s_exp, 1)

            def out_hi(b, g):
                n = A_OTJ + g
                act.wait_ge(a_job, A_JOBS * b + n + 1)
                A.activation(k_hi[:, g, :], gen[n % 2][:, 0:S], ACT.Identity, bias=ch_bias[:, 2, g:g + 1]).then_inc(a_hi, 1)

            def keys(b, half):
                act.wait_ge(w_job, W_JOBS * b + W_X1J + half + 1)
                wait(act, w_yr, 2 * b + half)
                A.activation(w_key[:].rearrange("p c t -> p (c t)"), pw[:], ACT.Copy).then_inc(w_free, 1)

            def carry_exps(b, half):
                act.wait_ge(w_diff, 4 * b + 2 * half + 1)
                for i in range(HC):
                    c = HC * half + i
                    e = A.activation(w_e1[:, i, :], w_e1[:, i, :], ACT.Exp, bias=decay[:, c:c + 1])
                e.then_inc(w_carry, 1)
                act.wait_ge(w_diff, 4 * b + 2 * half + 2)
                A.activation(w_e2[:, :, 1:S + 1], w_e2[:, :, 1:S + 1], ACT.Exp).then_inc(w_carry, 1)

            def now_exps(b, half):
                act.wait_ge(w_min, 2 * b + half + 1)
                A.activation(w_key[:], w_key[:], ACT.Exp)
                A.activation(w_d[:], w_d[:], ACT.Exp).then_inc(w_now, 1)

            def x_split_hi(b):
                act.wait_ge(load_xr, 16 * (b + 1))
                wait(act, f_job, F_JOBS * (b - 2) + F_KTJ) if not isinstance(b, int) or b >= 2 else None
                wait(act, a_job, A_JOBS * (b - 1) + A_VJ + 2)
                A.activation(xt_hi[:], x_raw[:], ACT.Copy).then_inc(xt_hi_ready, 1)

            def iteration(t, do_a, w2, do_f, w1, prefetch):
                if do_a:
                    for j, (dst, which, job) in enumerate(((q_hi, 0, A_QJ), (k_hi, 1, A_KJ))):
                        if which == 1:
                            wait(act, w_yr, 2 * t)
                        for n in range(2):
                            act.wait_ge(a_job, A_JOBS * t + job + n + 1)
                            for i in range(2):
                                c = 2 * n + i
                                e = A.activation(dst[:, c, :], gen[(job + n) % 2][:, S * i:S * (i + 1)],
                                                 ACT.Identity, bias=ch_bias[:, which, c:c + 1])
                            e.then_inc(a_hi, 1)
                    for i in range(2, NG + 4):
                        if i < NG + 2:
                            exps(t, i - 2, a_sk, a_exp)
                        if i >= 4:
                            out_hi(t, i - 4)
                        if i == 4 and w2:
                            x2_split_hi(t - 1)
                if not do_a and w2:
                    x2_split_hi(t - 1)
                b = t - 1
                if do_f:
                    for n in range(2):
                        act.wait_ge(f_job, F_JOBS * b + F_QJ + n + 1)
                        A.activation(q_hi[:, 2 * n:2 * n + 2, :].rearrange("p c t -> p (c t)"),
                                     gen[(F_QJ + n) % 2][:], ACT.Copy).then_inc(f_hi, 1)
                    act.wait_ge(g_ready, b + 1)
                    for c in range(TT):
                        e = A.activation(g_exp[:, c, :], logit[:, c, :], ACT.Exp, bias=g_nmax[:, c:c + 1],
                                         accum_out=g_sum[:, c:c + 1])
                    e.then_inc(g_summed, 1)
                if w1:
                    keys(t, 0)
                    carry_exps(t, 0)
                if do_f:
                    exps(b, 0, f_sk, f_exp)
                if w1:
                    now_exps(t, 0)
                if prefetch:
                    x_split_hi(t + 1)
                if do_f:
                    exps(b, 1, f_sk, f_exp)
                if w1:
                    keys(t, 1)
                    carry_exps(t, 1)
                if do_f:
                    exps(b, 2, f_sk, f_exp)
                if w1:
                    now_exps(t, 1)
                if do_f:
                    exps(b, 3, f_sk, f_exp)

            def x2_split_hi(b):
                for half in range(2):
                    n = W_X2J + half
                    act.wait_ge(w_job, W_JOBS * b + n + 1)
                    A.activation(xt_hi[:, HC * half:HC * (half + 1), :].rearrange("p c t -> p (c t)"), pw[:],
                                 ACT.Copy).then_inc(x2_hi, 1)

            act.wait_ge(load_c, 16 * 5)
            A.activation(gate_hi[:], gate_raw[:], ACT.Copy).then_inc(w_split_hi, 1)
            A.activation(decay[:], decay[:], ACT.Exp).then_inc(act_0, 1)
            act.wait_ge(act_0, 1)
            A.activation(decay[:], decay[:], ACT.Copy, scale=-1.0).then_inc(act_0, 1)
            act.wait_ge(act_0, 2)
            x_split_hi(0)
            for n in range(NW * CC):
                act.wait_ge(load_w[n % 4], 16 * (n // 4 + 1))
                A.activation(w_hi[:, n // CC, n % CC, :],
                             slot(n),
                             ACT.Copy).then_inc(w_split_hi, 1)
            iteration(0, True, False, False, True, True)
            iteration(1, True, True, True, True, True)
            with act.Fori(2, NB - 1) as t:
                iteration(t, True, True, True, True, True)
            iteration(NB - 1, True, True, True, True, False)
            iteration(NB, False, True, True, False, False)

        DVE_A, DVE_W, DVE_F = 9, 5, 29

        @block.vector
        def _(dve):
            def maxima(b, g, s_sq, s_max):
                for i in range(3):
                    n = 3 * g + i
                    dve.wait_ge(s_sq, TILES * b + n + 1)
                    if i == 0:
                        src, dst = sq[n % 2][:].rearrange("p (h k) -> p h k", h=HG), neg_max[:, g % 2, 0:HG]
                    else:
                        src = sq[n % 2][:].rearrange("p (h k) -> p h k", h=2)
                        dst = neg_max[:, g % 2, HG + 2 * (i - 1):HG + 2 * i]
                    V.tensor_reduce(dst, src, AX.X, ALU.max, negate=True).then_inc(s_max, 1)

            def split_max(ch, b, g, job, jobs, s_job, s_free, mrow):
                n = job + g
                dve.wait_ge(s_job, jobs * b + n + 1)
                if g >= 1:
                    dve.wait_ge(mrow[g - 1], 64 * (b + 1))
                src = gen[n % 2][0:TT * HG, 0:P]
                ch.link(V.tensor_copy(max_hi[:], src))
                V.tensor_tensor(max_lo[:], src, max_hi[:].bitcast(f32), ALU.subtract)\
                    .then_inc(s_free, 1)

            def normalise(ch, b, g, s_po, s_norm, dst):
                dve.wait_ge(s_po, NG * b + g + 1)
                o = po[:, 0:TT * HG * (HD + 1)].rearrange("p (n d) -> p n d", d=HD + 1)
                ch.link(V.reciprocal(o_rec[:], o[:, :, HD]))
                last_op = V.tensor_tensor(dst, o[:, :, 0:HD],
                                          o_rec[:].unsqueeze(2).to_broadcast([P, TT * HG, HD]), ALU.mult)
                last_op.then_inc(s_norm, 1)

            def ln_stats(ch, n, buf):
                for c in range(TT):
                    i = V.bn_stats(stats[:, n, c, :], buf[:, c, :])
                ch.link(i)
                V.memset(spare[:], 0.0)
                for c in range(TT):
                    i = V.bn_aggr(meanvar[:, n, c, :], stats[:, n, c, :])
                i.then_inc(ln_stat[n], 1)

            def ln_apply(n, b, buf, ready):
                dve.wait_ge(ln_rstd[n], b + 1)
                for c in range(TT):
                    i = V.tensor_scalar(buf[:, c, :], buf[:, c, :], meanvar[:, n, c, 0:1], rstd[:, n, c:c + 1],
                                        ALU.subtract, ALU.mult)
                i.then_inc(ready, 1)

            def running_max(ch, b, half):
                dve.wait_ge(w_free, W_JOBS * b + W_X1J + half + 1)
                wait(dve, w_den, 4 * b + 2 * half)
                for i in range(HC):
                    c = HC * half + i
                    s = V.tensor_tensor_scan(w_max[:, i, 1:S + 1], decay[:, c:c + 1].to_broadcast([P, S]),
                                             w_key[:, i, :], START_MAX, ALU.add, ALU.max)
                s.then_inc(w_pp, 1)

            def differences(ch, b, half):
                dve.wait_ge(w_pp, 2 * b + half + 1)
                wait(dve, w_den, 4 * b + 2 * half)
                for i in range(HC):
                    c = HC * half + i
                    s = V.scalar_tensor_tensor(w_d[:, i, :], w_key[:, i, :], first[:, c:c + 1],
                                               w_max[:, i, 0:S], ALU.add, ALU.subtract)
                ch.link(s)
                dve.wait_ge(w_diff, 4 * b + 2 * half + 2)
                ch.link(V.tensor_scalar(w_key[:], w_d[:], -1.0, 0.0, ALU.mult, ALU.min))
                V.tensor_scalar(w_d[:], w_d[:], 0.0, None, ALU.min).then_inc(w_min, 1)

            def sums(b, half):
                dve.wait_ge(w_carry, 4 * b + 2 * half + 2)
                dve.wait_ge(w_evr, 2 * b + half + 1)
                for i in range(HC):
                    V.tensor_tensor_scan(w_e2[:, i, 1:S + 1], w_e1[:, i, :], w_e2[:, i, 1:S + 1], 0.0,
                                         ALU.mult, ALU.add)
                    s = V.tensor_tensor_scan(w_max[:, i, 1:S + 1], w_e1[:, i, :], w_ev[:, i, :], 0.0,
                                             ALU.mult, ALU.add)
                s.then_inc(w_scan, 1)

            def divide(b, half):
                dve.wait_ge(w_den, 4 * b + 2 * half + 1)
                V.reciprocal(w_key[:], w_key[:]).then_inc(w_rec, 1)

            def second_residual(ch, b):
                wait(dve, stored, 16 * b)
                for half in range(2):
                    dve.wait_ge(w_job, W_JOBS * b + W_YJ + half + 1)
                    cols = slice(HC * P * half, HC * P * (half + 1))
                    i = V.tensor_tensor(xb[:, :, cols], pw[:].rearrange("p (c d) -> p c d", c=TT), xa[:, :, cols],
                                        ALU.add)
                    i.then_inc(w_free, 1)
                dve.wait_ge(w_free, W_JOBS * b + W_YJ + 2)
                ln_stats(ch, 1, xb)

            def x2_split_lo(b):
                for half in range(2):
                    n = W_X2J + half
                    dve.wait_ge(x2_hi, 2 * b + half + 1)
                    part = slice(HC * half, HC * (half + 1))
                    V.tensor_tensor(xt_lo[:, part, :].rearrange("p c t -> p (c t)"), pw[:],
                                    xt_hi[:, part, :].rearrange("p c t -> p (c t)").bitcast(f32), ALU.subtract)\
                        .then_inc(w_free, 1)

            def stage_a(t, w2, ln3):
                ch = Chain(dve, dve_a, DVE_A, t)
                for dst, hi, which, job, at in ((q_lo, q_hi, 0, A_QJ, 0), (k_lo, k_hi, 1, A_KJ, 2)):
                    for n in range(2):
                        dve.wait_ge(a_hi, 8 * t + at + n + 1)
                        for i in range(2):
                            c = 2 * n + i
                            o = V.scalar_tensor_tensor(dst[:, c, :], gen[(job + n) % 2][:, S * i:S * (i + 1)],
                                                       ch_bias[:, which, c:c + 1], hi[:, c, :].bitcast(f32),
                                                       ALU.add, ALU.subtract)
                        o.then_inc(a_free, 1)
                if ln3:
                    ln_apply(2, t - 2, xb, x3_ready)
                for c in range(TT):
                    dve.wait_ge(a_job, A_JOBS * t + A_VJ + c + 1)
                    V.tensor_copy(v_a[:, c, :, 0:HD],
                                  gen[(A_VJ + c) % 2][:].rearrange("p (h d) -> p h d", h=NH)).then_inc(a_free, 1)
                for i in range(NG + 4):
                    if i == 0 and w2:
                        chw = Chain(dve, dve_w, DVE_W, t - 1)
                        chw.n = DVE_W - 1
                        second_residual(chw, t - 1)
                    if i < NG:
                        maxima(t, i, a_sq, a_max)
                    if 1 <= i <= NG:
                        split_max(ch, t, i - 1, A_MJ, A_JOBS, a_job, a_free, a_mrow)
                    if i == 2 and w2:
                        ln_apply(1, t - 1, xb, x2_ready)
                    if i >= 4:
                        n = A_OTJ + i - 4
                        dve.wait_ge(a_hi, 8 * t + 4 + i - 4 + 1)
                        V.scalar_tensor_tensor(k_lo[:, i - 4, :], gen[n % 2][:, 0:S], ch_bias[:, 2, i - 4:i - 3],
                                               k_hi[:, i - 4, :].bitcast(f32), ALU.add, ALU.subtract)\
                            .then_inc(a_free, 1)
                    if 3 <= i < NG + 3:
                        if i > 3:
                            dve.wait_ge(a_job, A_JOBS * t + A_OTJ + i - 3)
                        normalise(ch, t, i - 3, a_po, a_norm, o_tok[:].rearrange("p c (h d) -> p (c h) d", h=HG))
                    if i == 4 and w2:
                        x2_split_lo(t - 1)
                dve.wait_ge(xa_ready, t + 1)
                for c in range(TT):
                    n = A_WOJ + c
                    dve.wait_ge(a_job, A_JOBS * t + n + 1)
                    V.tensor_tensor(xa[:, c, :], gen[n % 2][:], xa[:, c, :], ALU.add).then_inc(a_free, 1)
                dve.wait_ge(a_free, A_JOBS * (t + 1))
                ln_stats(ch, 0, xa)
                ch.close()

            def gating(ch, b):
                n = F_GATEJ
                dve.wait_ge(f_job, F_JOBS * b + n + 1)
                wait(dve, g_summed, b)
                V.tensor_copy(logit[:], gen[n % 2][:, 0:TT * NH].rearrange("p (c h) -> p c h", c=TT)).then_inc(f_free, 1)
                dve.wait_ge(f_free, F_JOBS * b + n + 1)
                ch.mark(V.tensor_reduce(g_max[:], logit[:], AX.X, ALU.max))
                V.tensor_reduce(g_nmax[:], logit[:], AX.X, ALU.max, negate=True).then_inc(g_ready, 1)
                ch.wait()
                ch.link(V.tensor_tensor(g_eq[:], logit[:], g_max[:].unsqueeze(2).to_broadcast([P, TT, NH]), ALU.is_equal))
                ch.link(V.tensor_tensor(g_rank[:], g_eq[:], rank[:].unsqueeze(1).to_broadcast([P, TT, NH]), ALU.mult))
                ch.link(V.tensor_reduce(g_top[:], g_rank[:], AX.X, ALU.max))
                ch.link(V.tensor_tensor(g_ind[:], g_rank[:], g_top[:].unsqueeze(2).to_broadcast([P, TT, NH]), ALU.is_equal))
                dve.wait_ge(g_summed, b + 1)
                ch.link(V.reciprocal(g_val[:], g_sum[:]))

            def pick(ch, b, job, c, dst):
                n = job + c
                dve.wait_ge(f_job, F_JOBS * b + n + 1)
                V.tensor_tensor(picked, gen[n % 2][:].rearrange("p (h d) -> p h d", h=NH),
                                g_ind[:, c, :].unsqueeze(2).to_broadcast([P, NH, HD]), ALU.mult).then_inc(f_free, 1)
                dve.wait_ge(f_free, F_JOBS * b + n + 1)
                ch.link(V.tensor_reduce(dst[:, c, :], picked.rearrange("p h d -> p d h"), AX.X, ALU.add))

            def stage_f(b, w1, x1_of):
                ch = Chain(dve, dve_f, DVE_F, b)
                for n in range(2):
                    dve.wait_ge(f_hi, 2 * b + n + 1)
                    V.tensor_tensor(q_lo[:, 2 * n:2 * n + 2, :].rearrange("p c t -> p (c t)"), gen[(F_QJ + n) % 2][:],
                                    q_hi[:, 2 * n:2 * n + 2, :].rearrange("p c t -> p (c t)").bitcast(f32),
                                    ALU.subtract).then_inc(f_free, 1)
                gating(ch, b)
                if w1:
                    ln_apply(0, x1_of, xa, x1_ready)
                for c in range(TT):
                    pick(ch, b, F_KJ, c, k_sel)
                    ch.link(V.tensor_copy(k3[:, c, 0:3:2, :], k_sel[:, c, :].unsqueeze(1).to_broadcast([P, 2, HD])))
                    ch.link(V.tensor_tensor(k3[:, c, 1, :], k_sel[:, c, :], k3[:, c, 0, :].bitcast(f32), ALU.subtract))
                assert ch.n == DVE_F_K3, ch.n
                for c in range(TT):
                    pick(ch, b, F_VJ, c, v_sel)
                    ch.link(V.tensor_scalar(v_f[:, c, 0:HD], v_sel[:, c, :], g_val[:, c:c + 1], None, ALU.mult))
                n = F_KTJ
                dve.wait_ge(f_job, F_JOBS * b + n + 1)
                V.tensor_copy(kf_stack[0:3 * HD, :], gen[n % 2][0:3 * HD, 0:S]).then_inc(f_free, 1)
                if w1:
                    chw = Chain(dve, dve_w, DVE_W, x1_of)
                    running_max(chw, x1_of, 0)
                for i in range(NG + 3):
                    if i < NG:
                        maxima(b, i, f_sq, f_max)
                    if 1 <= i <= NG:
                        split_max(ch, b, i - 1, F_MJ, F_JOBS, f_job, f_free, f_mrow)
                    if w1:
                        w1_step(chw, x1_of, i)
                    if i >= 3:
                        g = i - 3
                        normalise(ch, b, g, f_po, f_norm, o_tok[:].rearrange("p c (h d) -> p (c h) d", h=HG))
                        dve.wait_ge(f_norm, NG * b + g + 1)
                        cols = slice(P * g, P * (g + 1))
                        r = V.tensor_tensor(xb[:, :, cols], xb[:, :, cols],
                                            o_tok[:], ALU.add)
                        ch.link(r)
                ln_stats(ch, 2, xb)
                ch.close()

            def w1_step(chw, b, i):
                if i == 0:
                    differences(chw, b, 0)
                if i == 1:
                    sums(b, 0)
                if i == 2:
                    divide(b, 0)
                if i == 4:
                    running_max(chw, b, 1)
                    differences(chw, b, 1)
                if i == 5:
                    sums(b, 1)
                if i == 6:
                    divide(b, 1)

            dve.wait_ge(w_split_hi, 1)
            V.tensor_tensor(gate_lo[:], gate_raw[:], gate_hi[:].bitcast(f32), ALU.subtract)
            V.memset(eps[:], EPS)
            V.memset(minus_half[:], -0.5).then_inc(consts, 1)
            for n in range(NW * CC):
                dve.wait_ge(w_split_hi, n + 2)
                V.tensor_tensor(w_lo[:, n // CC, n % CC, :],
                                slot(n),
                                w_hi[:, n // CC, n % CC, :].bitcast(f32), ALU.subtract).then_inc(w_split_lo, 1)
            V.memset(v_a[:, :, :, HD:HD + 1], 1.0)
            V.memset(v_f[:, :, HD:HD + 1], 1.0)
            V.memset(k_stack[3 * HD:3 * HD + 2, :, :].bitcast(f32), 1.0)
            V.memset(kf_stack[3 * HD:3 * HD + 2, :].bitcast(f32), 1.0)
            V.memset(w_max[:, :, 0:1], START_MAX)
            V.memset(w_e2[:, :, 0:1], 0.0).then_inc(w_split_lo, 1)
            dve.wait_ge(consts, CONSTS)
            dve.wait_ge(act_0, 2)

            def w1_alone(b):
                ln_apply(0, b, xa, x1_ready)
                chw = Chain(dve, dve_w, DVE_W, b)
                running_max(chw, b, 0)
                for i in range(NG + 3):
                    w1_step(chw, b, i)

            stage_a(0, False, False)
            w1_alone(0)
            stage_a(1, True, False)
            stage_f(0, True, 1)
            with dve.Fori(2, NB) as t:
                stage_a(t, True, True)
                stage_f(t - 1, True, t)
            chw = Chain(dve, dve_w, DVE_W, NB - 1)
            chw.n = DVE_W - 1
            ln_apply(2, NB - 2, xb, x3_ready)
            second_residual(chw, NB - 1)
            ln_apply(1, NB - 1, xb, x2_ready)
            x2_split_lo(NB - 1)
            stage_f(NB - 1, False, None)
            ln_apply(2, NB - 1, xb, x3_ready)

        @block.gpsimd
        def _(pool):
            def inverse_std(b, n):
                pool.wait_ge(ln_stat[n], b + 1)
                G.tensor_tensor(var_eps[:, n, :], meanvar[:, n, :, 1], eps[:], ALU.add).then_inc(pool_ln[n], 1)
                pool.wait_ge(pool_ln[n], b + 1)
                G.tensor_tensor(rstd[:, n, :], var_eps[:, n, :], minus_half[:], ALU.pow).then_inc(ln_rstd[n], 1)

            def add_bo(b):
                pool.wait_ge(load_xa, 16 * (b + 1))
                for c in range(TT):
                    i = G.tensor_tensor(xa[:, c, :], xa[:, c, :], bo_row[:], ALU.add)
                i.then_inc(xa_ready, 1)

            def x_split_lo(b):
                pool.wait_ge(xt_hi_ready, b + 1)
                G.tensor_tensor(xt_lo[:], x_raw[:], xt_hi[:].bitcast(f32), ALU.subtract).then_inc(xt_ready, 1)

            def recurrence(b, half):
                ch = Chain(pool, pool_w, 6, b)
                ch.n = 3 * half
                now, after = slice(1, S + 1), slice(0, S)
                pool.wait_ge(w_pp, 2 * b + half + 1)
                G.tensor_tensor(w_e1[:], w_max[:, :, after], w_max[:, :, now], ALU.subtract).then_inc(w_diff, 1)
                G.tensor_tensor(w_e2[:, :, now], w_key[:], w_max[:, :, now], ALU.subtract).then_inc(w_diff, 1)
                pool.wait_ge(w_carry, 4 * b + 2 * half + 2)
                pool.wait_ge(load_v, 16 * (2 * b + half + 1))
                G.tensor_tensor(w_ev[:], w_e2[:, :, now], w_val[:], ALU.mult).then_inc(w_evr, 1)
                pool.wait_ge(w_scan, 2 * b + half + 1)
                pool.wait_ge(w_now, 2 * b + half + 1)
                ch.mark(G.tensor_tensor(w_e1[:], w_key[:], w_max[:, :, after], ALU.mult))
                ch.mark(G.tensor_tensor(w_ev[:], w_d[:], w_val[:], ALU.mult))
                ch.mark(G.tensor_tensor(w_key[:], w_key[:], w_e2[:, :, after], ALU.mult))
                ch.wait()
                G.tensor_tensor(w_key[:], w_key[:], w_d[:], ALU.add).then_inc(w_den, 1)
                G.tensor_tensor(w_ev[:], w_e1[:], w_ev[:], ALU.add).then_inc(w_den, 1)
                pool.wait_ge(w_den, 4 * b + 2 * half + 2)
                pool.wait_ge(w_rec, 2 * b + half + 1)
                wait(pool, w_job, W_JOBS * (b - 1) + W_YJ + half + 1)
                G.tensor_tensor(w_y[:, half, :, :], w_ev[:], w_key[:], ALU.mult).then_inc(w_yr, 1)

            G.memset(ident[:], 0.0).then_inc(zero_done, 1)
            G.memset(mask_qk[:], 0.0).then_inc(zero_done, 1)
            G.memset(mask_kq[:], 0.0).then_inc(zero_done, 1)
            G.iota(rank[:], pattern=[[-1, NH]], base=NH, channel_multiplier=0,
                   allow_small_or_imprecise_dtypes=True).then_inc(zero_done, 1)
            pool.wait_ge(zero_done, 4)
            G.affine_select(out=ident[:], in_=ident[:], compare_op=ALU.not_equal, fill=1.0, base=0,
                            pattern=[[-1, P]], channel_multiplier=1).then_inc(pool_0, 1)
            G.affine_select(out=mask_qk[:], in_=mask_qk[:], compare_op=ALU.is_ge, fill=MASKED, base=0,
                            pattern=[[-1, P]], channel_multiplier=1).then_inc(pool_0, 1)
            G.affine_select(out=mask_kq[:], in_=mask_kq[:], compare_op=ALU.is_ge, fill=MASKED, base=0,
                            pattern=[[1, P]], channel_multiplier=-1).then_inc(pool_0, 1)
            pool.wait_ge(pool_0, 3)
            G.tensor_copy(ident_b[:], ident[:]).then_inc(consts, 1)
            pool.wait_ge(consts, CONSTS)
            x_split_lo(0)
            add_bo(0)
            inverse_std(0, 0)
            recurrence(0, 0)
            x_split_lo(1)
            recurrence(0, 1)

            def iteration(t, prefetch, ln3):
                inverse_std(t - 1, 1)
                add_bo(t)
                inverse_std(t, 0)
                recurrence(t, 0)
                if prefetch:
                    x_split_lo(t + 1)
                recurrence(t, 1)
                inverse_std(t - 1, 2)

            with pool.Fori(1, NB - 1) as t:
                iteration(t, True, True)
            iteration(NB - 1, False, True)
            inverse_std(NB - 1, 1)
            inverse_std(NB - 1, 2)


def kernel(**inputs):
    import numpy as np
    import concourse.bacc as bacc
    from concourse.bass_utils import run_bass_kernel_spmd as run

    a = {n: np.asarray(v) for n, v in inputs.items()}

    def quadrants(w):
        return w.reshape(NG, CC, HD, -1).transpose(1, 0, 2, 3).reshape(D, -1)

    wqkv = a["L0_ffn_W_qkv"]
    mats = [quadrants(a["L0_attn_Wq"]), quadrants(a["L0_attn_Wk"]), a["L0_attn_Wv"], a["L0_attn_Wo"],
            quadrants(wqkv[0:D]), wqkv[D:2 * D], wqkv[2 * D:3 * D]]
    arrays = {
        "x": a["x"],
        "xT": a["x"].transpose(0, 2, 1),
        "ctxT": a["ctx_2048"].transpose(0, 2, 1),
        "weights": np.stack([m.T.reshape(CC, P, D) for m in mats]),
        "gate": a["L0_ffn_W_gate"].T,
        "ch_bias": np.stack([quadrants(a["L0_attn_bq"].reshape(D, 1)).reshape(CC, P).T,
                             quadrants(a["L0_attn_bk"].reshape(D, 1)).reshape(CC, P).T,
                             a["L0_attn_bv"].reshape(CC, P).T], axis=1),
        "row_bias": np.broadcast_to(a["L0_attn_bo"], (P, D)),
        "decay": a["L0_xattn_time_decay"].reshape(CC, P).T,
        "first": a["L0_xattn_time_first"].reshape(CC, P).T,
    }
    nc = bacc.Bacc("TRN2", target_bir_lowering=False, num_devices=1)
    fed, args = {}, []
    for name, v in arrays.items():
        v = np.ascontiguousarray(v)
        fed[f"in_{name}"] = v
        args.append(nc.dram_tensor(f"in_{name}", v.shape, mybir.dt.from_np(v.dtype), kind="ExternalInput").ap())
    out = nc.dram_tensor("out_y", (NB, S, D), mybir.dt.float32, kind="ExternalOutput").ap()
    build(nc, *args, out)
    return run(nc, [fed], core_ids=[0]).results[0]["out_y"]
```

```python
import concourse.bass as bass
from concourse import mybir
from contextlib import ExitStack

NB, S, D = 16, 256, 512
NH, HD = 16, 32
P = 128
CC = D // P
TT = S // P
NG = 4
HG = NH // NG
SCALE = float(HD) ** -0.5
EPS = 1e-5
MASKED = -1e30
START_MAX = -1e38

W_Q, W_K, W_V, W_O, W_FQ, W_FK, W_FV = range(7)
NW = 7

PA_JOBS, PA_Q, PA_K, PA_V, PA_WO = 8, 0, 2, 4, 6
PF_JOBS, PF_Q, PF_K, PF_KT, PF_V = 7, 0, 2, 4, 5
A_JOBS, A_M, A_OT = 8, (0, 1, 3, 5), (2, 4, 6, 7)
F_JOBS, F_M = 4, (0, 1, 2, 3)
F_LINKS, F_LINK_K3, F_LINK_PICKED = 29, 12, 16
A_LINKS, W_LINKS = 9, 9
TILES = 3 * NG
W_JOBS, W_X1J, W_YJ, W_X2J, W_GATE = 7, 0, 2, 4, 6
CONSTS = 2


def build(nc, x_d, xT_d, ctxT_d, weights_d, gate_d, ch_bias_d, row_bias_d, decay_d, first_d, out_d):
    f32, f32r, bf16 = mybir.dt.float32, mybir.dt.float32r, mybir.dt.bfloat16
    ALU, ACT, AX = mybir.AluOpType, mybir.ActivationFunctionType, mybir.AxisListType
    V, A, T, G = nc.vector, nc.scalar, nc.tensor, nc.gpsimd

    ctx = ExitStack()
    with ctx:
        def sb(name, shape, dt=f32):
            return ctx.enter_context(nc.sbuf_tensor(name, shape, dt))

        def overlaid(name, size, *tensors):
            base = nc.sbuf_base
            sb(name, [P, size // 4])
            return [nc.alloc_sbuf_tensor_at(n, shape, dt, offset=base + at) for n, shape, dt, at in tensors]

        def pb(name):
            return ctx.enter_context(nc.psum_tensor(name, [P, 512], f32))

        def sem(name):
            return ctx.enter_context(nc.semaphore(name))

        w_hi = sb("w_hi", [P, NW, CC, D], f32r)
        w_lo = sb("w_lo", [P, NW, CC, D], f32r)
        gate = sb("gate", [P, CC, NH])
        q_stack = sb("q_stack", [P, NH, S], f32r)
        HC = CC // 2
        half, behind = HC * S * 4, NH * S * 4 // 2
        k_stack, w_key, w_e1, w_d, w_ev = overlaid(
            "k_stack_region", NH * S * 4, ("k_stack", [P, NH, S], f32r, 0),
            ("w_key", [P, HC, S], f32, behind), ("w_e1", [P, HC, S], f32, behind + half),
            ("w_d", [P, HC, S], f32, behind + 2 * half), ("w_ev", [P, HC, S], f32, behind + 3 * half))
        kf_stack = sb("kf_stack", [P, S], f32r)
        q_hi, x_raw = overlaid("q_region", CC * S * 4,
                               ("q_hi", [P, CC, S], f32r, 0),
                               ("x_raw", [P, CC, S], f32, 0))
        q_lo = sb("q_lo", [P, CC, S], f32r)
        k_hi = sb("k_hi", [P, CC, S], f32r)
        k_lo = sb("k_lo", [P, CC, S], f32r)
        xt_hi = sb("xt_hi", [P, CC, S], f32r)
        xt_lo = sb("xt_lo", [P, CC, S], f32r)
        xa = sb("xa", [P, TT, D])
        xb = sb("xb", [P, TT, D])
        v_a = sb("v_a", [P, TT, NH, HD + 1])
        v_f = sb("v_f", [P, TT, HD + 1])
        prob0 = sb("prob0", [P, HG, S])
        prob1 = sb("prob1", [P, HG, P])
        o_tok = sb("o_tok", [P, TT, HG * HD])
        bo_row = sb("bo_row", [P, D])
        ch_bias = sb("ch_bias", [P, 3, CC])
        neg_max = sb("neg_max", [P, HG, TT])
        neg_parts = sb("neg_parts", [P, 2, HG, TT], f32r)
        max_rows = sb("max_rows", [2 * HG * TT, P], f32r)
        ident = sb("ident", [P, P])
        ident_b = sb("ident_b", [P, P], bf16)
        mask_qk = sb("mask_qk", [P, P], bf16)
        mask_kq = sb("mask_kq", [P, P], bf16)
        o_rec = sb("o_rec", [P, TT * HG])
        w_val = sb("w_val", [P, HC, S])
        picked = w_val[:].rearrange("p c t -> p (c t)").rearrange("p (h d) -> p h d", h=NH)
        w_max = sb("w_max", [P, HC, S + 1])
        w_e2 = sb("w_e2", [P, HC, S + 1])
        w_y = sb("w_y", [P, 2, HC, S])
        decay = sb("decay", [P, CC])
        first = sb("first", [P, CC])
        stats = sb("stats", [P, 3, TT, 6])
        spare = sb("spare", [P, 3])
        spare_pool = sb("spare_pool", [P, 1])
        eps = sb("eps", [P, TT])
        meanvar = sb("meanvar", [P, 3, TT, 2])
        var_eps = sb("var_eps", [P, 3, TT])
        rstd = sb("rstd", [P, 3, TT])
        minus_half = sb("minus_half", [P, TT])
        logit = sb("logit", [P, TT, NH])
        g_max = sb("g_max", [P, TT])
        g_nmax = sb("g_nmax", [P, TT])
        g_eq = sb("g_eq", [P, TT, NH])
        g_rank = sb("g_rank", [P, TT, NH])
        g_top = sb("g_top", [P, TT])
        g_ind = sb("g_ind", [P, TT, NH])
        g_exp = sb("g_exp", [P, TT, NH])
        g_sum = sb("g_sum", [P, TT])
        g_val = sb("g_val", [P, TT])
        rank = sb("rank", [P, NH])
        k_sel = sb("k_sel", [P, TT, HD])
        v_sel = sb("v_sel", [P, TT, HD])
        k3 = sb("k3", [P, TT, 3, HD], f32r)

        pp = pb("pp")
        pt = pb("pt")
        sq = [pb("sq0"), pb("sq1")]
        sk = [pb("sk0"), pb("sk1")]
        po = pb("po")
        pw = pb("pw")

        load_w = [sem(f"load_w{i}") for i in range(4)]
        load_c = sem("load_c")
        load_xr, load_xa, load_v = sem("load_xr"), sem("load_xa"), [sem(f"load_v{i}") for i in range(2)]
        w_split_hi, w_split_lo = sem("w_split_hi"), sem("w_split_lo")
        consts, zero_done = sem("consts"), sem("zero_done")
        xt_hi_ready, xt_ready, xa_ready = sem("xt_hi_ready"), sem("xt_ready"), sem("xa_ready")
        a_job, a_free, f_job, f_free = sem("a_job"), sem("a_free"), sem("f_job"), sem("f_free")
        a_sq, a_max, f_sq, f_max = sem("a_sq"), sem("a_max"), sem("f_sq"), sem("f_max")
        a_neg, f_neg = sem("a_neg"), sem("f_neg")
        a_sk, a_exp, f_sk, f_exp = sem("a_sk"), sem("a_exp"), sem("f_sk"), sem("f_exp")
        a_po, a_norm, f_po, f_norm = sem("a_po"), sem("a_norm"), sem("f_po"), sem("f_norm")
        pa_job, pa_free, pf_job, pf_free = sem("pa_job"), sem("pa_free"), sem("pf_job"), sem("pf_free")
        pa_hi, pf_hi, ot_hi, w_ones = sem("pa_hi"), sem("pf_hi"), sem("ot_hi"), sem("w_ones")
        a_stk = [sem(f"a_stk{g}") for g in range(NG)]
        f_stk = [sem(f"f_stk{g}") for g in range(NG)]
        a_mrow = [sem(f"a_mrow{g}") for g in range(NG)]
        f_mrow = [sem(f"f_mrow{g}") for g in range(NG)]
        w_job, w_free, x2_hi = sem("w_job"), sem("w_free"), sem("x2_hi")
        w_pp, w_diff, w_carry, w_min = sem("w_pp"), sem("w_diff"), sem("w_carry"), sem("w_min")
        w_evr, w_scan, w_now, w_den = sem("w_evr"), sem("w_scan"), sem("w_now"), sem("w_den")
        w_rec, w_yr = sem("w_rec"), sem("w_yr")
        ln_stat = [sem(f"ln_stat{n}") for n in range(3)]
        ln_rstd = [sem(f"ln_rstd{n}") for n in range(3)]
        x1_ready, x2_ready, x3_ready = sem("x1_ready"), sem("x2_ready"), sem("x3_ready")
        g_ready, g_summed = sem("g_ready"), sem("g_summed")
        stored = sem("stored")
        dve_a, dve_w, dve_f, dve_0 = sem("dve_a"), sem("dve_w"), sem("dve_f"), sem("dve_0")
        pool_w, pool_0 = sem("pool_w"), sem("pool_0")
        pool_ln = [sem(f"pool_ln{n}") for n in range(3)]
        act_0 = sem("act_0")

        def slot(n):
            if n % 4 < 2:
                return prob0[:].rearrange("p h q -> p (h q)")[:, D * (n % 2):D * (n % 2 + 1)]
            return xb[:, n % 2, :]

        def wait(eng, s, value):
            if not isinstance(value, int) or value > 0:
                eng.wait_ge(s, value)

        class Chain:
            def __init__(self, eng, s, per, b):
                self.eng, self.s, self.base, self.per, self.n = eng, s, per * b, per, 0

            def mark(self, ins):
                ins.then_inc(self.s, 1)
                self.n += 1

            def wait(self):
                self.eng.wait_ge(self.s, self.base + self.n)

            def link(self, ins):
                self.mark(ins)
                self.wait()

            def close(self):
                assert self.n == self.per, self.n

        def values_done(b):
            return PA_JOBS * NB if isinstance(b, int) and b == NB else PA_JOBS * b + PA_WO

        block = ctx.enter_context(nc.Block())

        @block.sync
        def _(sp):
            def load_xr_of(b, stk, count):
                for g in range(NG):
                    wait(sp, stk[g], count)
                sp.dma_start(x_raw[:], xT_d[b].rearrange("(c p) t -> p c t", p=P)).then_inc(load_xr, 16)

            def stack(dst, lo, src, g, s):
                sp.dma_start(dst[lo:lo + HD, HG * g:HG * (g + 1), :].bitcast(f32),
                             src[HD * g:HD * (g + 1), :, :].bitcast(f32)).then_inc(s, 16)

            def stack_max(b, g, job, jobs, s_free, mrow):
                wait(sp, s_free, jobs * b + job[g] + 1)
                sp.dma_start(q_stack[3 * HD:3 * HD + 2, HG * g:HG * (g + 1), :].bitcast(f32),
                             max_rows[:].bitcast(f32)).then_inc(mrow[g], 16)

            def load_ctx(b, c):
                if c >= HC:
                    wait(sp, w_den, 2 * (CC * b + c - HC + 1))
                sp.dma_start(w_val[:, c % HC, :], ctxT_d[b, P * c:P * (c + 1)]).then_inc(load_v[c % HC], 16)

            def store(b):
                wait(sp, x3_ready, b + 1)
                sp.dma_start(out_d[b].rearrange("(c p) d -> p c d", p=P), xb[:]).then_inc(stored, 16)

            def q_stacks(b, jobs, job, s_free, groups, s_used, used, stk):
                if jobs is not None:
                    wait(sp, s_free, jobs * b + job + 2)
                for g in groups:
                    if s_used is not None:
                        wait(sp, s_used, used + 3 * (g + 1))
                    for lo, src in ((0, q_hi), (HD, q_hi), (2 * HD, q_lo)):
                        stack(q_stack, lo, src, g, stk[g])

            def k_stacks(b, groups):
                if groups[0] == 0:
                    wait(sp, pa_free, PA_JOBS * b + PA_K + 2)
                else:
                    wait(sp, w_ones, b + 1)
                for g in groups:
                    for lo, src in ((0, k_hi), (HD, k_lo), (2 * HD, k_hi)):
                        stack(k_stack, lo, src, g, a_stk[g])

            def max_a(b, g):
                stack_max(b, g, A_M, A_JOBS, a_free, a_mrow)

            def max_f(b, g):
                stack_max(b, g, F_M, F_JOBS, f_free, f_mrow)

            def iteration(t, do_a, prev, nxt):
                b = t - 1
                if do_a:
                    max_a(t, 1)
                if prev and not (isinstance(t, int) and t < 2):
                    store(t - 2)
                if do_a:
                    max_a(t, 2)
                    wait(sp, x2_ready, t)
                    sp.dma_start(xa[:], x_d[t].rearrange("(c p) d -> p c d", p=P)).then_inc(load_xa, 16)
                if prev:
                    q_stacks(b, PF_JOBS, PF_Q, pf_free, range(NG - 1), a_sk if do_a else None, TILES * t, f_stk)
                if do_a:
                    max_a(t, 3)
                if prev:
                    q_stacks(b, None, None, None, range(NG - 1, NG), a_sk if do_a else None, TILES * t, f_stk)
                if nxt:
                    if prev:
                        load_xr_of(t + 1, f_stk, 48 * t)
                    else:
                        load_xr_of(t + 1, a_stk, 96 * (t + 1))
                if prev:
                    max_f(b, 0)
                    if do_a:
                        wait(sp, dve_f, F_LINKS * b + F_LINK_PICKED)
                if do_a:
                    load_ctx(t, 0)
                    load_ctx(t, 1)
                if prev:
                    max_f(b, 1)
                    max_f(b, 2)
                if nxt:
                    q_stacks(t + 1, PA_JOBS, PA_Q, pa_free, range(NG - 2), f_sk if prev else None, TILES * b, a_stk)
                if prev:
                    max_f(b, 3)
                if nxt:
                    k_stacks(t + 1, range(2))
                    q_stacks(t + 1, None, None, None, range(NG - 2, NG - 1), f_sk if prev else None, TILES * b, a_stk)
                if do_a:
                    load_ctx(t, 2)
                    load_ctx(t, 3)
                if nxt:
                    q_stacks(t + 1, None, None, None, range(NG - 1, NG), f_sk if prev else None, TILES * b, a_stk)
                    max_a(t + 1, 0)
                    k_stacks(t + 1, range(2, NG))

            sp.dma_start(ch_bias[:], ch_bias_d).then_inc(load_c, 16)
            sp.dma_start(decay[:], decay_d).then_inc(load_c, 16)
            sp.dma_start(first[:], first_d).then_inc(load_c, 16)
            sp.dma_start(bo_row[:], row_bias_d).then_inc(load_c, 16)
            sp.dma_start(gate[:], gate_d.rearrange("(c p) h -> p c h", p=P)).then_inc(load_c, 16)
            load_xr_of(0, a_stk, 0)
            for n in range(NW * CC):
                wait(sp, w_split_lo, n - 3)
                sp.dma_start(slot(n), weights_d[n // CC, n % CC]).then_inc(load_w[n % 4], 16)
            q_stacks(0, PA_JOBS, PA_Q, pa_free, range(NG), None, 0, a_stk)
            k_stacks(0, range(2))
            max_a(0, 0)
            k_stacks(0, range(2, NG))
            iteration(0, True, False, True)
            iteration(1, True, True, True)
            with sp.Fori(2, NB - 1) as t:
                iteration(t, True, True, True)
            iteration(NB - 1, True, True, False)
            iteration(NB, False, True, False)
            store(NB - 1)
            sp.wait_ge(stored, 16 * NB)

        @block.tensor
        def _(pe):
            def products(out, lhs, rhs):
                for c in range(CC):
                    (lh, ll), (rh, rl) = lhs(c), rhs(c)
                    T.matmul(out, lh, rh, start=(c == 0), stop=False, skip_group_check=True)
                    T.matmul(out, lh, rl, start=False, stop=False, skip_group_check=True)
                    mm = T.matmul(out, ll, rh, start=False, stop=(c == CC - 1), skip_group_check=True)
                return mm

            def weight(w, lo, n):
                return lambda c: (w_hi[:, w, c, lo:lo + n], w_lo[:, w, c, lo:lo + n])

            def tokens(lo, n, hi_t=xt_hi, lo_t=xt_lo):
                return lambda c: (hi_t[:, c, lo:lo + n], lo_t[:, c, lo:lo + n])

            def channels_out(w, pair):
                for i in range(2):
                    mm = products(pp[:, S * i:S * (i + 1)], weight(w, P * (2 * pair + i), P), tokens(0, S))
                return mm

            def tokens_out(bank, w, c, hi_t=xt_hi, lo_t=xt_lo):
                return products(bank[:, 0:D], tokens(P * c, P, hi_t, lo_t), weight(w, 0, D))

            def scores_sq(b, g, tiles, stk, per, key, s_sq, s_max):
                if tiles[0] == 0:
                    pe.wait_ge(stk[g], per * (b + 1))
                for i in tiles:
                    n = 3 * g + i
                    if n >= 2:
                        pe.wait_ge(s_max, TILES * b + n - 1)
                    out = sq[n % 2]
                    if i == 0:
                        for k in range(HG):
                            h = HG * g + k
                            T.matmul(out[:, P * k:P * (k + 1)], q_stack[0:3 * HD, h, 0:P], key(h, 0, P, 3 * HD),
                                     start=(k == 0), stop=False, skip_group_check=True)
                        for k in range(HG):
                            mm = T.matmul(out[:, P * k:P * (k + 1)], ident_b[:], mask_qk[:],
                                          start=False, stop=(k == HG - 1), skip_group_check=True)
                    else:
                        for k in range(2):
                            h = HG * g + 2 * (i - 1) + k
                            T.matmul(out[:, S * k:S * (k + 1)], q_stack[0:3 * HD, h, P:S], key(h, 0, S, 3 * HD),
                                     start=(k == 0), stop=False, skip_group_check=True)
                        for k in range(2):
                            mm = T.matmul(out[:, S * k + P:S * (k + 1)], ident_b[:], mask_qk[:],
                                          start=False, stop=(k == 1), skip_group_check=True)
                    mm.then_inc(s_sq, 1)

            def max_transpose(s_neg, count, s_before, before, s_job):
                pe.wait_ge(s_neg, count)
                wait(pe, s_before, before)
                T.transpose(pt[0:2 * HG * TT, 0:P], neg_parts[:].rearrange("p a h c -> p (a h c)").bitcast(f32),
                            ident[:]).then_inc(s_job, 1)

            def scores_sk(b, g, tiles, mrow, key, s_sk, s_exp):
                if tiles[0] == 0:
                    pe.wait_ge(mrow[g], 16 * (b + 1))
                rows = 3 * HD + 2
                for i in tiles:
                    n = 3 * g + i
                    if n >= 2:
                        pe.wait_ge(s_exp, TILES * b + n - 1)
                    out = sk[n % 2]
                    if i < 2:
                        for k in range(2):
                            h = HG * g + 2 * i + k
                            T.matmul(out[:, S * k:S * (k + 1)], key(h, 0, P, rows), q_stack[0:rows, h, :],
                                     start=(k == 0), stop=False, skip_group_check=True)
                        for k in range(2):
                            mm = T.matmul(out[:, S * k:S * k + P], ident_b[:], mask_kq[:],
                                          start=False, stop=(k == 1), skip_group_check=True)
                    else:
                        for k in range(HG):
                            h = HG * g + k
                            T.matmul(out[:, P * k:P * (k + 1)], key(h, P, P, rows), q_stack[0:rows, h, P:S],
                                     start=(k == 0), stop=False, skip_group_check=True)
                        for k in range(HG):
                            mm = T.matmul(out[:, P * k:P * (k + 1)], ident_b[:], mask_kq[:],
                                          start=False, stop=(k == HG - 1), skip_group_check=True)
                    mm.then_inc(s_sk, 1)

            def values(b, g, value, s_exp, s_norm, s_po):
                if g:
                    pe.wait_ge(s_norm, NG * b + g)
                pe.wait_ge(s_exp, TILES * b + 3 * (g + 1))
                out = po[:, 0:TT * HG * (HD + 1)].rearrange("p (c h d) -> p c h d", c=TT, h=HG)
                for k in range(HG):
                    h = HG * g + k
                    T.matmul(out[:, 0, k, :], prob0[:, k, 0:P], value(0, h),
                             start=True, stop=True, skip_group_check=True)
                    T.matmul(out[:, 1, k, :], prob0[:, k, P:S], value(0, h),
                             start=True, stop=False, skip_group_check=True)
                    mm = T.matmul(out[:, 1, k, :], prob1[:, k, :], value(1, h),
                                  start=False, stop=True, skip_group_check=True)
                mm.then_inc(s_po, 1)

            def out_transpose(b, g, s_before, before):
                pe.wait_ge(a_norm, NG * b + g + 1)
                wait(pe, s_before, before)
                for c in range(TT):
                    mm = T.transpose(pt[:, P * c:P * (c + 1)], o_tok[:, c, :], ident[:])
                mm.then_inc(a_job, 1)

            def x_transpose(b, job, half, src, ready, count):
                pe.wait_ge(ready, count)
                wait(pe, w_free, W_JOBS * b + job + half)
                for i in range(HC):
                    for c in range(TT):
                        ch = P * (HC * half + i)
                        mm = T.transpose(pw[:, S * i + P * c:S * i + P * (c + 1)], src[:, c, ch:ch + P], ident[:])
                mm.then_inc(w_job, 1)

            def y_transpose(b, half):
                pe.wait_ge(w_yr, CC * b + HC * (half + 1))
                pe.wait_ge(w_free, W_JOBS * b + W_YJ + half)
                for c in range(TT):
                    for i in range(HC):
                        at = HC * P * c + P * i
                        mm = T.transpose(pw[:, at:at + P], w_y[:, half, i, P * c:P * (c + 1)], ident[:])
                mm.then_inc(w_job, 1)

            def key_a(h, lo, n, rows):
                return k_stack[0:rows, h, lo:lo + n]

            def key_f(h, lo, n, rows):
                return kf_stack[0:rows, lo:lo + n]

            def project_a(b, job):
                if job == PA_Q:
                    pe.wait_ge(xt_ready, b + 1)
                if job == PA_WO:
                    wait(pe, pf_free, PF_JOBS * b)
                    pe.wait_ge(a_free, A_JOBS * (b + 1))
                if job != PA_WO:
                    wait(pe, pa_free, PA_JOBS * b + job)
                if job < PA_K:
                    mm = channels_out(W_Q, job - PA_Q)
                elif job < PA_V:
                    mm = channels_out(W_K, job - PA_K)
                elif job < PA_WO:
                    mm = tokens_out(pp, W_V, job - PA_V)
                else:
                    mm = tokens_out(pp, W_O, job - PA_WO, k_hi, k_lo)
                mm.then_inc(pa_job, 1)

            def project_f(b, job):
                if job == PF_Q:
                    pe.wait_ge(w_free, W_JOBS * b + W_X2J + 2)
                    pe.wait_ge(pa_free, values_done(b + 1))
                else:
                    pe.wait_ge(pf_free, PF_JOBS * b + job)
                if job < PF_K:
                    mm = channels_out(W_FQ, job - PF_Q)
                elif job < PF_KT:
                    mm = tokens_out(pp, W_FK, job - PF_K)
                elif job == PF_KT:
                    pe.wait_ge(dve_f, F_LINKS * b + F_LINK_K3)
                    for c in range(TT):
                        mm = T.transpose(pp[0:3 * HD, P * c:P * (c + 1)],
                                         k3[:, c, :, :].rearrange("p a d -> p (a d)").bitcast(f32), ident[:])
                else:
                    mm = tokens_out(pp, W_FV, job - PF_V)
                mm.then_inc(pf_job, 1)

            def gate_logits(b):
                pe.wait_ge(w_free, W_JOBS * b + W_GATE)
                for c in range(TT):
                    for k in range(CC):
                        for part in (xt_hi, xt_lo):
                            mm = T.matmul(pw[:, NH * c:NH * (c + 1)], part[:, k, P * c:P * (c + 1)].bitcast(f32),
                                          gate[:, k, :], start=(k == 0 and part is xt_hi),
                                          stop=(k == CC - 1 and part is xt_lo), skip_group_check=True)
                mm.then_inc(w_job, 1)

            def sq_a(b, g, *tiles):
                scores_sq(b, g, tiles, a_stk, 96, key_a, a_sq, a_max)

            def sq_f(b, g, *tiles):
                scores_sq(b, g, tiles, f_stk, 48, key_f, f_sq, f_max)

            def sk_a(b, g, *tiles):
                scores_sk(b, g, tiles, a_mrow, key_a, a_sk, a_exp)

            def sk_f(b, g, *tiles):
                scores_sk(b, g, tiles, f_mrow, key_f, f_sk, f_exp)

            def max_a(b, g, s_before=None, before=0):
                if s_before is None:
                    s_before, before = a_free, A_JOBS * b + A_M[g]
                max_transpose(a_neg, NG * b + g + 1, s_before, before, a_job)

            def max_f(b, g, s_before=None, before=0):
                if s_before is None:
                    s_before, before = f_free, F_JOBS * b + g
                max_transpose(f_neg, NG * b + g + 1, s_before, before, f_job)

            def values_a(b, g):
                values(b, g, value_a, a_exp, a_norm, a_po)

            def values_f(b, g):
                values(b, g, value_f, f_exp, f_norm, f_po)

            def iteration(t, do_a, prev, nxt):
                b = t - 1
                a_done = t + 1 if do_a else NB
                if do_a:
                    sq_a(t, 1, 0, 1)
                    sk_a(t, 0, 2)
                    project_a(t, PA_V + 1)
                    sq_a(t, 1, 2)
                if prev:
                    y_transpose(b, 1)
                if do_a:
                    max_a(t, 1)
                    pe.wait_ge(pa_free, values_done(t))
                    wait(pe, f_norm, NG * b)
                    wait(pe, a_norm, NG * t)
                    values_a(t, 0)
                    sk_a(t, 1, 0, 1)
                    sq_a(t, 2, 0, 1)
                    sk_a(t, 1, 2)
                    out_transpose(t, 0, a_free, A_JOBS * t + A_OT[0])
                    sq_a(t, 2, 2)
                if prev:
                    x_transpose(b, W_X2J, 0, xb, x2_ready, t)
                if do_a:
                    values_a(t, 1)
                    max_a(t, 2)
                if prev:
                    x_transpose(b, W_X2J, 1, xb, x2_ready, t)
                    project_f(b, PF_Q)
                if do_a:
                    sk_a(t, 2, 0, 1)
                    sq_a(t, 3, 0, 1)
                    sk_a(t, 2, 2)
                    out_transpose(t, 1, a_free, A_JOBS * t + A_OT[1])
                if prev:
                    project_f(b, PF_Q + 1)
                if do_a:
                    sq_a(t, 3, 2)
                if prev:
                    gate_logits(b)
                    project_f(b, PF_K)
                if do_a:
                    max_a(t, 3)
                    values_a(t, 2)
                if prev:
                    project_f(b, PF_K + 1)
                if do_a:
                    sk_a(t, 3, 0, 1)
                    out_transpose(t, 2, a_free, A_JOBS * t + A_OT[2])
                if prev:
                    project_f(b, PF_KT)
                if do_a:
                    sk_a(t, 3, 2)
                if prev:
                    pe.wait_ge(pf_free, PF_JOBS * b + PF_KT + 1)
                    wait(pe, a_max, TILES * a_done)
                    sq_f(b, 0, 0, 1)
                    project_f(b, PF_V)
                    sq_f(b, 0, 2)
                if do_a:
                    values_a(t, 3)
                if prev:
                    max_f(b, 0, a_free, A_JOBS * t + A_OT[2] + 1 if do_a else A_JOBS * NB)
                    project_f(b, PF_V + 1)
                    wait(pe, a_exp, TILES * a_done)
                    sk_f(b, 0, 0, 1)
                    sq_f(b, 1, 0, 1)
                    sk_f(b, 0, 2)
                if do_a:
                    if prev:
                        wait(pe, f_free, F_JOBS * b + 1)
                    out_transpose(t, 3, a_free, A_JOBS * t + A_OT[3])
                if prev:
                    sq_f(b, 1, 2)
                    wait(pe, a_norm, NG * a_done)
                    pe.wait_ge(dve_f, F_LINKS * b + F_LINK_PICKED + 1)
                    values_f(b, 0)
                    max_f(b, 1, a_free, A_JOBS * a_done)
                if do_a:
                    project_a(t, PA_WO)
                if prev:
                    sk_f(b, 1, 0, 1)
                if do_a:
                    project_a(t, PA_WO + 1)
                if prev:
                    sq_f(b, 2, 0, 1)
                    sk_f(b, 1, 2)
                if nxt:
                    project_a(t + 1, PA_Q)
                if prev:
                    sq_f(b, 2, 2)
                if do_a:
                    x_transpose(t, W_X1J, 0, xa, x1_ready, t + 1)
                if prev:
                    values_f(b, 1)
                    max_f(b, 2)
                if nxt:
                    project_a(t + 1, PA_Q + 1)
                if prev:
                    sk_f(b, 2, 0, 1)
                    sq_f(b, 3, 0, 1)
                    sk_f(b, 2, 2)
                if nxt:
                    project_a(t + 1, PA_K)
                if prev:
                    sq_f(b, 3, 2)
                if do_a:
                    x_transpose(t, W_X1J, 1, xa, x1_ready, t + 1)
                if prev:
                    values_f(b, 2)
                    max_f(b, 3)
                if nxt:
                    project_a(t + 1, PA_K + 1)
                if prev:
                    sk_f(b, 3, 0, 1)
                    sk_f(b, 3, 2)
                if nxt:
                    project_a(t + 1, PA_V)
                    wait(pe, f_max, TILES * t)
                    wait(pe, a_max, TILES * (t + 1))
                    sq_a(t + 1, 0, 0, 1)
                if prev:
                    values_f(b, 3)
                if nxt:
                    sq_a(t + 1, 0, 2)
                if do_a:
                    y_transpose(t, 0)
                if nxt:
                    if prev:
                        max_a(t + 1, 0, f_free, F_JOBS * t)
                        pe.wait_ge(f_exp, TILES * t)
                    else:
                        max_a(t + 1, 0)
                        wait(pe, a_exp, TILES * (t + 1))
                    sk_a(t + 1, 0, 0, 1)

            def value_a(c, h):
                return v_a[:, c, h, :]

            def value_f(c, h):
                return v_f[:, c, :]

            pe.wait_ge(consts, CONSTS)
            pe.wait_ge(w_split_lo, NW * CC + 1)
            for job in range(PA_V + 1):
                project_a(0, job)
            sq_a(0, 0, 0, 1, 2)
            max_a(0, 0)
            sk_a(0, 0, 0, 1)
            iteration(0, True, False, True)
            iteration(1, True, True, True)
            with pe.Fori(2, NB - 1) as t:
                iteration(t, True, True, True)
            iteration(NB - 1, True, True, False)
            iteration(NB, False, True, False)

        @block.scalar
        def _(act):
            def exps(b, g, tiles, s_sk, s_exp):
                for i in tiles:
                    n = 3 * g + i
                    act.wait_ge(s_sk, TILES * b + n + 1)
                    if i < 2:
                        dst = prob0[:, 2 * i:2 * i + 2, :].rearrange("p h q -> p (h q)")
                    else:
                        dst = prob1[:].rearrange("p h q -> p (h q)")
                    A.activation(dst, sk[n % 2][:], ACT.Exp, scale=SCALE).then_inc(s_exp, 1)

            def exps_a(b, g, *tiles):
                exps(b, g, tiles, a_sk, a_exp)

            def exps_f(b, g, *tiles):
                exps(b, g, tiles, f_sk, f_exp)

            def out_hi(b, g):
                act.wait_ge(a_job, A_JOBS * b + A_OT[g] + 1)
                if g == 0:
                    for stk in a_stk:
                        act.wait_ge(stk, 96 * (b + 1))
                A.activation(k_hi[:, g, :], pt[:, 0:S], ACT.Identity, bias=ch_bias[:, 2, g:g + 1])\
                    .then_inc(ot_hi, 1)

            def carry_exps(b, c):
                act.wait_ge(w_diff, CC * b + c + 1)
                A.activation(w_e1[:, c % HC, :], w_e1[:, c % HC, :], ACT.Exp, bias=decay[:, c:c + 1])
                act.wait_ge(w_min, CC * b + c + 1)
                A.activation(w_e2[:, c % HC, 1:S + 1], w_e2[:, c % HC, 1:S + 1], ACT.Exp).then_inc(w_carry, 1)

            def now_exps(b, c):
                A.activation(w_key[:, c % HC, :], w_key[:, c % HC, :], ACT.Exp)
                A.activation(w_d[:, c % HC, :], w_d[:, c % HC, :], ACT.Exp).then_inc(w_now, 1)

            def all_exps(b, c):
                carry_exps(b, c)
                now_exps(b, c)

            def x_split_hi(b):
                act.wait_ge(load_xr, 16 * (b + 1))
                wait(act, pf_job, PF_JOBS * (b - 1))
                wait(act, pa_job, PA_JOBS * (b - 1) + PA_WO)
                A.activation(xt_hi[:], x_raw[:], ACT.Copy).then_inc(xt_hi_ready, 1)

            def qk_hi(b, job):
                which, n = (0, job - PA_Q) if job < PA_K else (1, job - PA_K)
                dst = (q_hi, k_hi)[which]
                act.wait_ge(pa_job, PA_JOBS * b + job + 1)
                for i in range(2):
                    c = 2 * n + i
                    e = A.activation(dst[:, c, :], pp[:, S * i:S * (i + 1)], ACT.Identity,
                                     bias=ch_bias[:, which, c:c + 1])
                e.then_inc(pa_hi, 1)

            def value_out(b, c):
                act.wait_ge(pa_job, PA_JOBS * b + PA_V + c + 1)
                A.activation(v_a[:, c, :, 0:HD], pp[:].rearrange("p (h d) -> p h d", h=NH), ACT.Copy)\
                    .then_inc(pa_free, 1)

            def fq_hi(b, n):
                act.wait_ge(pf_job, PF_JOBS * b + PF_Q + n + 1)
                A.activation(q_hi[:, 2 * n:2 * n + 2, :].rearrange("p c t -> p (c t)"), pp[:], ACT.Copy)\
                    .then_inc(pf_hi, 1)

            def gate_sums(b):
                act.wait_ge(g_ready, b + 1)
                for c in range(TT):
                    e = A.activation(g_exp[:, c, :], logit[:, c, :], ACT.Exp, bias=g_nmax[:, c:c + 1],
                                     accum_out=g_sum[:, c:c + 1])
                e.then_inc(g_summed, 1)

            def iteration(t, do_a, prev, nxt):
                b = t - 1
                if do_a:
                    exps_a(t, 0, 2)
                    value_out(t, 1)
                    exps_a(t, 1, 0, 1)
                    exps_a(t, 1, 2)
                    out_hi(t, 0)
                if prev:
                    x2_split_hi(b)
                if do_a:
                    exps_a(t, 2, 0, 1)
                if prev:
                    fq_hi(b, 0)
                if do_a:
                    exps_a(t, 2, 2)
                    out_hi(t, 1)
                if prev:
                    fq_hi(b, 1)
                    gate_sums(b)
                if do_a:
                    exps_a(t, 3, 0, 1)
                    out_hi(t, 2)
                    exps_a(t, 3, 2)
                if prev:
                    exps_f(b, 0, 0, 1)
                    exps_f(b, 0, 2)
                if nxt:
                    x_split_hi(t + 1)
                if do_a:
                    out_hi(t, 3)
                if prev:
                    exps_f(b, 1, 0, 1)
                    exps_f(b, 1, 2)
                if nxt:
                    qk_hi(t + 1, PA_Q)
                    qk_hi(t + 1, PA_Q + 1)
                if do_a:
                    carry_exps(t, 0)
                if prev:
                    exps_f(b, 2, 0, 1)
                    exps_f(b, 2, 2)
                if do_a:
                    carry_exps(t, 1)
                    now_exps(t, 0)
                    now_exps(t, 1)
                if nxt:
                    qk_hi(t + 1, PA_K)
                    qk_hi(t + 1, PA_K + 1)
                if prev:
                    exps_f(b, 3, 0, 1)
                    exps_f(b, 3, 2)
                if do_a:
                    all_exps(t, 2)
                    all_exps(t, 3)
                if nxt:
                    value_out(t + 1, 0)
                    exps_a(t + 1, 0, 0, 1)

            def x2_split_hi(b):
                for half in range(2):
                    n = W_X2J + half
                    act.wait_ge(w_job, W_JOBS * b + n + 1)
                    A.activation(xt_hi[:, HC * half:HC * (half + 1), :].rearrange("p c t -> p (c t)"), pw[:],
                                 ACT.Copy).then_inc(x2_hi, 1)

            act.wait_ge(load_c, 16 * 5)
            A.activation(decay[:], decay[:], ACT.Exp).then_inc(act_0, 1)
            act.wait_ge(act_0, 1)
            A.activation(decay[:], decay[:], ACT.Copy, scale=-1.0).then_inc(act_0, 1)
            act.wait_ge(act_0, 2)
            x_split_hi(0)
            for n in range(NW * CC):
                act.wait_ge(load_w[n % 4], 16 * (n // 4 + 1))
                A.activation(w_hi[:, n // CC, n % CC, :],
                             slot(n),
                             ACT.Copy).then_inc(w_split_hi, 1)
            for job in range(PA_V):
                qk_hi(0, job)
            value_out(0, 0)
            exps_a(0, 0, 0, 1)
            iteration(0, True, False, True)
            iteration(1, True, True, True)
            with act.Fori(2, NB - 1) as t:
                iteration(t, True, True, True)
            iteration(NB - 1, True, True, False)
            iteration(NB, False, True, False)

        @block.vector
        def _(dve):
            def maxima(ch, b, g, tiles, s_sq, s_max, s_neg):
                for i in tiles:
                    n = 3 * g + i
                    dve.wait_ge(s_sq, TILES * b + n + 1)
                    if i == 0:
                        src, dst = sq[n % 2][:].rearrange("p (h k) -> p h k", h=HG), neg_max[:, :, 0]
                    else:
                        src = sq[n % 2][:].rearrange("p (h k) -> p h k", h=2)
                        dst = neg_max[:, 2 * (i - 1):2 * i, 1]
                    V.tensor_reduce(dst, src, AX.X, ALU.max, negate=True).then_inc(s_max, 1)
                if tiles[-1] != 2:
                    return
                dve.wait_ge(s_max, TILES * b + 3 * (g + 1))
                ch.link(V.tensor_copy(neg_parts[:, 0, :, :], neg_max[:]))
                V.tensor_tensor(neg_parts[:, 1, :, :], neg_max[:], neg_parts[:, 0, :, :].bitcast(f32),
                                ALU.subtract).then_inc(s_neg, 1)

            def rows(b, g, job, jobs, s_job, s_free, s_read, read):
                dve.wait_ge(s_job, jobs * b + job[g] + 1)
                wait(dve, s_read, read)
                V.tensor_copy(max_rows[:], pt[0:2 * HG * TT, 0:P]).then_inc(s_free, 1)

            def maxima_a(ch, b, g, *tiles):
                maxima(ch, b, g, tiles or (0, 1, 2), a_sq, a_max, a_neg)

            def maxima_f(ch, b, g, *tiles):
                maxima(ch, b, g, tiles or (0, 1, 2), f_sq, f_max, f_neg)

            def rows_a(b, g, s_read=None, read=0):
                if g:
                    s_read, read = a_mrow[g - 1], 16 * (b + 1)
                rows(b, g, A_M, A_JOBS, a_job, a_free, s_read, read)

            def rows_f(b, g, s_read=None, read=0):
                if g:
                    s_read, read = f_mrow[g - 1], 16 * (b + 1)
                rows(b, g, F_M, F_JOBS, f_job, f_free, s_read, read)

            def normalise(ch, b, g, s_po, s_norm):
                dve.wait_ge(s_po, NG * b + g + 1)
                o = po[:, 0:TT * HG * (HD + 1)].rearrange("p (n d) -> p n d", d=HD + 1)
                ch.link(V.reciprocal(o_rec[:], o[:, :, HD]))
                last_op = V.tensor_tensor(o_tok[:].rearrange("p c (h d) -> p (c h) d", h=HG), o[:, :, 0:HD],
                                          o_rec[:].unsqueeze(2).to_broadcast([P, TT * HG, HD]), ALU.mult)
                last_op.then_inc(s_norm, 1)

            def ln_stats(ch, n, buf):
                for c in range(TT):
                    i = V.bn_stats(stats[:, n, c, :], buf[:, c, :])
                ch.link(i)
                V.memset(spare[:, n:n + 1], 0.0)
                for c in range(TT):
                    i = V.bn_aggr(meanvar[:, n, c, :], stats[:, n, c, :])
                i.then_inc(ln_stat[n], 1)

            def ln_apply(n, b, src, dst, ready):
                dve.wait_ge(ln_rstd[n], b + 1)
                for c in range(TT):
                    i = V.tensor_scalar(dst[:, c, :], src[:, c, :], meanvar[:, n, c, 0:1], rstd[:, n, c:c + 1],
                                        ALU.subtract, ALU.mult)
                i.then_inc(ready, 1)

            def recurrence_start(ch, b, c):
                i, k = c % HC, pw[:, S * (c % HC):S * (c % HC + 1)]
                dve.wait_ge(w_job, W_JOBS * b + W_X1J + c // HC + 1)
                if c >= HC:
                    dve.wait_ge(w_den, 2 * (CC * b + c - HC + 1))
                V.tensor_tensor_scan(w_max[:, i, 1:S + 1], decay[:, c:c + 1].to_broadcast([P, S]), k,
                                     START_MAX, ALU.add, ALU.max).then_inc(w_pp, 1)
                dve.wait_ge(w_pp, CC * b + c + 1)
                ch.mark(V.scalar_tensor_tensor(w_d[:, i, :], k, first[:, c:c + 1], w_max[:, i, 0:S],
                                               ALU.add, ALU.subtract))
                e2 = V.tensor_tensor(w_e2[:, i, 1:S + 1], k, w_max[:, i, 1:S + 1], ALU.subtract)
                if i == HC - 1:
                    e2.then_inc(w_free, 1)
                if c >= HC:
                    dve.wait_ge(w_yr, CC * b + c - HC + 1)
                ch.wait()
                ch.link(V.tensor_scalar(w_key[:, i, :], w_d[:, i, :], -1.0, 0.0, ALU.mult, ALU.min))
                V.tensor_scalar(w_d[:, i, :], w_d[:, i, :], 0.0, None, ALU.min).then_inc(w_min, 1)

            def sums(b, c):
                i = c % HC
                dve.wait_ge(w_carry, CC * b + c + 1)
                dve.wait_ge(w_evr, CC * b + c + 1)
                V.tensor_tensor_scan(w_e2[:, i, 1:S + 1], w_e1[:, i, :], w_e2[:, i, 1:S + 1], 0.0,
                                     ALU.mult, ALU.add)
                V.tensor_tensor_scan(w_max[:, i, 1:S + 1], w_e1[:, i, :], w_ev[:, i, :], 0.0,
                                     ALU.mult, ALU.add).then_inc(w_scan, 1)

            def divide(b, c):
                dve.wait_ge(w_den, 2 * (CC * b + c) + 1)
                V.reciprocal(w_key[:, c % HC, :], w_key[:, c % HC, :]).then_inc(w_rec, 1)

            def second_residual(b, half):
                dve.wait_ge(w_job, W_JOBS * b + W_YJ + half + 1)
                cols = slice(HC * P * half, HC * P * (half + 1))
                V.tensor_tensor(xa[:, :, cols], pw[:].rearrange("p (c d) -> p c d", c=TT), xa[:, :, cols],
                                ALU.add).then_inc(w_free, 1)

            def second_stats(ch, b):
                dve.wait_ge(w_free, W_JOBS * b + W_YJ + 2)
                ln_stats(ch, 1, xa)

            def second_norm(b):
                wait(dve, stored, 16 * b)
                ln_apply(1, b, xa, xb, x2_ready)

            def x2_split_lo(b, half):
                dve.wait_ge(x2_hi, 2 * b + half + 1)
                part = slice(HC * half, HC * (half + 1))
                V.tensor_tensor(xt_lo[:, part, :].rearrange("p c t -> p (c t)"), pw[:],
                                xt_hi[:, part, :].rearrange("p c t -> p (c t)").bitcast(f32), ALU.subtract)\
                    .then_inc(w_free, 1)

            def qk_lo(b, job):
                which, n = (0, job - PA_Q) if job < PA_K else (1, job - PA_K)
                hi, lo = (q_hi, k_hi)[which], (q_lo, k_lo)[which]
                dve.wait_ge(pa_hi, 4 * b + job + 1)
                for i in range(2):
                    c = 2 * n + i
                    o = V.scalar_tensor_tensor(lo[:, c, :], pp[:, S * i:S * (i + 1)], ch_bias[:, which, c:c + 1],
                                               hi[:, c, :].bitcast(f32), ALU.add, ALU.subtract)
                o.then_inc(pa_free, 1)

            def fq_lo(b, n):
                dve.wait_ge(pf_hi, 2 * b + n + 1)
                V.tensor_tensor(q_lo[:, 2 * n:2 * n + 2, :].rearrange("p c t -> p (c t)"), pp[:],
                                q_hi[:, 2 * n:2 * n + 2, :].rearrange("p c t -> p (c t)").bitcast(f32),
                                ALU.subtract).then_inc(pf_free, 1)

            def out_lo(b, g):
                dve.wait_ge(ot_hi, NG * b + g + 1)
                V.scalar_tensor_tensor(k_lo[:, g, :], pt[:, 0:S], ch_bias[:, 2, g:g + 1],
                                       k_hi[:, g, :].bitcast(f32), ALU.add, ALU.subtract).then_inc(a_free, 1)

            def normalise_a(ch, b, g):
                if g:
                    dve.wait_ge(a_job, A_JOBS * b + A_OT[g - 1] + 1)
                normalise(ch, b, g, a_po, a_norm)

            def first_residual(b, c):
                if c == 0:
                    dve.wait_ge(xa_ready, b + 1)
                dve.wait_ge(pa_job, PA_JOBS * b + PA_WO + c + 1)
                V.tensor_tensor(xa[:, c, :], pp[:], xa[:, c, :], ALU.add).then_inc(pa_free, 1)

            def first_stats(ch, b):
                dve.wait_ge(pa_free, PA_JOBS * (b + 1))
                ln_stats(ch, 0, xa)

            def gating(ch, b):
                dve.wait_ge(w_job, W_JOBS * b + W_GATE + 1)
                V.tensor_copy(logit[:], pw[:, 0:TT * NH].rearrange("p (c h) -> p c h", c=TT)).then_inc(w_free, 1)
                dve.wait_ge(w_free, W_JOBS * (b + 1))
                ch.mark(V.tensor_reduce(g_max[:], logit[:], AX.X, ALU.max))
                V.tensor_reduce(g_nmax[:], logit[:], AX.X, ALU.max, negate=True).then_inc(g_ready, 1)
                ch.wait()
                ch.link(V.tensor_tensor(g_eq[:], logit[:], g_max[:].unsqueeze(2).to_broadcast([P, TT, NH]),
                                        ALU.is_equal))
                ch.link(V.tensor_tensor(g_rank[:], g_eq[:], rank[:].unsqueeze(1).to_broadcast([P, TT, NH]),
                                        ALU.mult))
                ch.link(V.tensor_reduce(g_top[:], g_rank[:], AX.X, ALU.max))
                ch.link(V.tensor_tensor(g_ind[:], g_rank[:], g_top[:].unsqueeze(2).to_broadcast([P, TT, NH]),
                                        ALU.is_equal))
                dve.wait_ge(g_summed, b + 1)
                ch.link(V.reciprocal(g_val[:], g_sum[:]))

            def pick(ch, b, job, c, dst):
                dve.wait_ge(pf_job, PF_JOBS * b + job + c + 1)
                V.tensor_tensor(picked, pp[:].rearrange("p (h d) -> p h d", h=NH),
                                g_ind[:, c, :].unsqueeze(2).to_broadcast([P, NH, HD]), ALU.mult).then_inc(pf_free, 1)
                dve.wait_ge(pf_free, PF_JOBS * b + job + c + 1)
                ch.link(V.tensor_reduce(dst[:, c, :], picked.rearrange("p h d -> p d h"), AX.X, ALU.add))

            def pick_key(ch, b, c):
                pick(ch, b, PF_K, c, k_sel)
                ch.link(V.tensor_copy(k3[:, c, 0:3:2, :], k_sel[:, c, :].unsqueeze(1).to_broadcast([P, 2, HD])))
                ch.link(V.tensor_tensor(k3[:, c, 1, :], k_sel[:, c, :], k3[:, c, 0, :].bitcast(f32), ALU.subtract))

            def pick_value(ch, b, c):
                pick(ch, b, PF_V, c, v_sel)
                ch.link(V.tensor_scalar(v_f[:, c, 0:HD], v_sel[:, c, :], g_val[:, c:c + 1], None, ALU.mult))

            def third_residual(ch, b, g):
                normalise(ch, b, g, f_po, f_norm)
                dve.wait_ge(f_norm, NG * b + g + 1)
                cols = slice(P * g, P * (g + 1))
                ch.link(V.tensor_tensor(xb[:, :, cols], xb[:, :, cols], o_tok[:], ALU.add))

            def iteration(t, do_a, prev, nxt):
                b = t - 1
                if do_a:
                    cha, chw = Chain(dve, dve_a, A_LINKS, t), Chain(dve, dve_w, W_LINKS, t)
                    cha.n = 1
                if prev:
                    chf, chy = Chain(dve, dve_f, F_LINKS, b), Chain(dve, dve_w, W_LINKS, b)
                    chy.n = W_LINKS - 1
                if nxt:
                    chn = Chain(dve, dve_a, A_LINKS, t + 1)
                if do_a:
                    maxima_a(cha, t, 1, 0, 1)
                if prev:
                    divide(b, 3)
                if do_a:
                    maxima_a(cha, t, 1, 2)
                if prev:
                    second_residual(b, 1)
                    second_stats(chy, b)
                    chy.close()
                if do_a:
                    rows_a(t, 1)
                if prev and not (isinstance(t, int) and t < 2):
                    ln_apply(2, t - 2, xb, xb, x3_ready)
                if do_a:
                    normalise_a(cha, t, 0)
                    maxima_a(cha, t, 2, 0, 1)
                if prev:
                    second_norm(b)
                if do_a:
                    out_lo(t, 0)
                    maxima_a(cha, t, 2, 2)
                if prev:
                    x2_split_lo(b, 0)
                if do_a:
                    rows_a(t, 2)
                    normalise_a(cha, t, 1)
                if prev:
                    x2_split_lo(b, 1)
                    fq_lo(b, 0)
                if do_a:
                    maxima_a(cha, t, 3, 0, 1)
                    out_lo(t, 1)
                if prev:
                    fq_lo(b, 1)
                if do_a:
                    maxima_a(cha, t, 3, 2)
                if prev:
                    gating(chf, b)
                if do_a:
                    rows_a(t, 3)
                if prev:
                    pick_key(chf, b, 0)
                if do_a:
                    normalise_a(cha, t, 2)
                if prev:
                    pick_key(chf, b, 1)
                if do_a:
                    out_lo(t, 2)
                if prev:
                    dve.wait_ge(pf_job, PF_JOBS * b + PF_KT + 1)
                    V.tensor_copy(kf_stack[0:3 * HD, :], pp[0:3 * HD, 0:S]).then_inc(pf_free, 1)
                    assert chf.n == F_LINK_K3
                    maxima_f(chf, b, 0)
                    pick_value(chf, b, 0)
                    rows_f(b, 0, a_mrow[NG - 1], 16 * (t + 1 if do_a else NB))
                if do_a:
                    normalise_a(cha, t, 3)
                if prev:
                    pick_value(chf, b, 1)
                    assert chf.n == F_LINK_PICKED + 1
                    maxima_f(chf, b, 1)
                if do_a:
                    out_lo(t, 3)
                if prev:
                    rows_f(b, 1)
                    third_residual(chf, b, 0)
                if do_a:
                    first_residual(t, 0)
                    first_residual(t, 1)
                    first_stats(cha, t)
                    cha.close()
                if prev:
                    maxima_f(chf, b, 2, 0, 1)
                if do_a:
                    ln_apply(0, t, xa, xa, x1_ready)
                if prev:
                    maxima_f(chf, b, 2, 2)
                if nxt:
                    qk_lo(t + 1, PA_Q)
                if prev:
                    rows_f(b, 2)
                if do_a:
                    recurrence_start(chw, t, 0)
                if nxt:
                    qk_lo(t + 1, PA_Q + 1)
                if prev:
                    third_residual(chf, b, 1)
                if do_a:
                    recurrence_start(chw, t, 1)
                if prev:
                    maxima_f(chf, b, 3)
                if do_a:
                    sums(t, 0)
                if nxt:
                    qk_lo(t + 1, PA_K)
                if prev:
                    rows_f(b, 3)
                if do_a:
                    sums(t, 1)
                if nxt:
                    qk_lo(t + 1, PA_K + 1)
                if prev:
                    third_residual(chf, b, 2)
                if do_a:
                    divide(t, 0)
                    recurrence_start(chw, t, 2)
                    divide(t, 1)
                    recurrence_start(chw, t, 3)
                if nxt:
                    maxima_a(chn, t + 1, 0)
                if do_a:
                    sums(t, 2)
                if nxt:
                    second_residual(t, 0)
                    if prev:
                        rows_a(t + 1, 0, f_mrow[NG - 1], 16 * t)
                    else:
                        rows_a(t + 1, 0, a_mrow[NG - 1], 16 * (t + 1))
                if prev:
                    third_residual(chf, b, 3)
                    ln_stats(chf, 2, xb)
                    chf.close()
                if do_a:
                    sums(t, 3)
                    divide(t, 2)
                    if not nxt:
                        second_residual(t, 0)

            V.memset(eps[:], EPS)
            V.memset(minus_half[:], -0.5).then_inc(consts, 1)
            for n in range(NW * CC):
                dve.wait_ge(w_split_hi, n + 1)
                V.tensor_tensor(w_lo[:, n // CC, n % CC, :],
                                slot(n),
                                w_hi[:, n // CC, n % CC, :].bitcast(f32), ALU.subtract).then_inc(w_split_lo, 1)
            V.memset(v_a[:, :, :, HD:HD + 1], 1.0)
            V.memset(v_f[:, :, HD:HD + 1], 1.0)
            V.memset(k_stack[3 * HD:3 * HD + 2, 0:NH // 2, :].bitcast(f32), 1.0)
            V.memset(kf_stack[3 * HD:3 * HD + 2, :].bitcast(f32), 1.0)
            V.memset(w_max[:, :, 0:1], START_MAX)
            V.memset(w_e2[:, :, 0:1], 0.0).then_inc(w_split_lo, 1)
            dve.wait_ge(consts, CONSTS)
            dve.wait_ge(act_0, 2)

            for job in range(PA_V):
                qk_lo(0, job)
            maxima_a(Chain(dve, dve_a, A_LINKS, 0), 0, 0)
            rows_a(0, 0)
            iteration(0, True, False, True)
            iteration(1, True, True, True)
            with dve.Fori(2, NB - 1) as t:
                iteration(t, True, True, True)
            iteration(NB - 1, True, True, False)
            iteration(NB, False, True, False)
            ln_apply(2, NB - 1, xb, xb, x3_ready)

        @block.gpsimd
        def _(pool):
            def inverse_std(b, n):
                pool.wait_ge(ln_stat[n], b + 1)
                G.tensor_tensor(var_eps[:, n, :], meanvar[:, n, :, 1], eps[:], ALU.add).then_inc(pool_ln[n], 1)
                pool.wait_ge(pool_ln[n], b + 1)
                G.tensor_tensor(rstd[:, n, :], var_eps[:, n, :], minus_half[:], ALU.pow).then_inc(ln_rstd[n], 1)

            def add_bo(b):
                pool.wait_ge(load_xa, 16 * (b + 1))
                for c in range(TT):
                    i = G.tensor_tensor(xa[:, c, :], xa[:, c, :], bo_row[:], ALU.add)
                i.then_inc(xa_ready, 1)

            def x_split_lo(b):
                pool.wait_ge(xt_hi_ready, b + 1)
                G.tensor_tensor(xt_lo[:], x_raw[:], xt_hi[:].bitcast(f32), ALU.subtract).then_inc(xt_ready, 1)

            now, after = slice(1, S + 1), slice(0, S)

            def difference(b, c):
                pool.wait_ge(w_pp, CC * b + c + 1)
                G.tensor_tensor(w_e1[:, c % HC, :], w_max[:, c % HC, after], w_max[:, c % HC, now],
                                ALU.subtract).then_inc(w_diff, 1)

            def weighted(b, c):
                i = c % HC
                pool.wait_ge(w_carry, CC * b + c + 1)
                pool.wait_ge(load_v[i], 16 * (HC * b + c // HC + 1))
                G.tensor_tensor(w_ev[:, i, :], w_e2[:, i, now], w_val[:, i, :], ALU.mult).then_inc(w_evr, 1)

            def products(b, c):
                i = c % HC
                ch = Chain(pool, pool_w, 3 * CC, b)
                ch.n = 3 * c
                pool.wait_ge(w_scan, CC * b + c + 1)
                pool.wait_ge(w_now, CC * b + c + 1)
                ch.mark(G.tensor_tensor(w_e1[:, i, :], w_key[:, i, :], w_max[:, i, after], ALU.mult))
                ch.mark(G.tensor_tensor(w_ev[:, i, :], w_d[:, i, :], w_val[:, i, :], ALU.mult))
                ch.mark(G.tensor_tensor(w_key[:, i, :], w_key[:, i, :], w_e2[:, i, after], ALU.mult))
                ch.wait()
                G.tensor_tensor(w_key[:, i, :], w_key[:, i, :], w_d[:, i, :], ALU.add).then_inc(w_den, 1)
                G.tensor_tensor(w_ev[:, i, :], w_e1[:, i, :], w_ev[:, i, :], ALU.add).then_inc(w_den, 1)

            def quotient(b, c):
                i = c % HC
                pool.wait_ge(w_den, 2 * (CC * b + c + 1))
                pool.wait_ge(w_rec, CC * b + c + 1)
                wait(pool, w_job, W_JOBS * (b - 1) + W_YJ + c // HC + 1)
                G.tensor_tensor(w_y[:, c // HC, i, :], w_ev[:, i, :], w_key[:, i, :], ALU.mult).then_inc(w_yr, 1)

            def ones_back(b):
                pool.wait_ge(w_yr, CC * (b + 1))
                G.tensor_tensor(spare_pool[0:1, :], eps[0:1, 0:1], eps[0:1, 0:1], ALU.add)
                G.memset(k_stack[3 * HD:3 * HD + 2, NH // 2:, :].bitcast(f32), 1.0).then_inc(w_ones, 1)
                pool.wait_ge(w_ones, b + 2)

            G.memset(ident[:], 0.0).then_inc(zero_done, 1)
            G.memset(mask_qk[:], 0.0).then_inc(zero_done, 1)
            G.memset(mask_kq[:], 0.0).then_inc(zero_done, 1)
            G.iota(rank[:], pattern=[[-1, NH]], base=NH, channel_multiplier=0,
                   allow_small_or_imprecise_dtypes=True).then_inc(zero_done, 1)
            pool.wait_ge(zero_done, 4)
            G.affine_select(out=ident[:], in_=ident[:], compare_op=ALU.not_equal, fill=1.0, base=0,
                            pattern=[[-1, P]], channel_multiplier=1).then_inc(pool_0, 1)
            G.affine_select(out=mask_qk[:], in_=mask_qk[:], compare_op=ALU.is_ge, fill=MASKED, base=0,
                            pattern=[[-1, P]], channel_multiplier=1).then_inc(pool_0, 1)
            G.affine_select(out=mask_kq[:], in_=mask_kq[:], compare_op=ALU.is_ge, fill=MASKED, base=0,
                            pattern=[[1, P]], channel_multiplier=-1).then_inc(pool_0, 1)
            pool.wait_ge(pool_0, 3)
            G.tensor_copy(ident_b[:], ident[:]).then_inc(consts, 1)
            pool.wait_ge(consts, CONSTS)
            G.memset(k_stack[3 * HD:3 * HD + 2, NH // 2:, :].bitcast(f32), 1.0).then_inc(w_ones, 1)
            pool.wait_ge(w_ones, 1)
            x_split_lo(0)

            def iteration(t, prev, nxt):
                if prev:
                    inverse_std(t - 1, 1)
                add_bo(t)
                if nxt:
                    x_split_lo(t + 1)
                inverse_std(t, 0)
                difference(t, 0)
                difference(t, 1)
                weighted(t, 0)
                weighted(t, 1)
                products(t, 0)
                products(t, 1)
                quotient(t, 0)
                difference(t, 2)
                quotient(t, 1)
                difference(t, 3)
                weighted(t, 2)
                weighted(t, 3)
                products(t, 2)
                if prev:
                    inverse_std(t - 1, 2)
                products(t, 3)
                quotient(t, 2)
                quotient(t, 3)
                ones_back(t)

            iteration(0, False, True)
            iteration(1, True, True)
            with pool.Fori(2, NB - 1) as t:
                iteration(t, True, True)
            iteration(NB - 1, True, False)
            inverse_std(NB - 1, 1)
            inverse_std(NB - 1, 2)


def kernel(**inputs):
    import numpy as np
    import concourse.bacc as bacc
    from concourse.bass_utils import run_bass_kernel_spmd as run

    a = {n: np.asarray(v) for n, v in inputs.items()}

    def quadrants(w):
        return w.reshape(NG, CC, HD, -1).transpose(1, 0, 2, 3).reshape(D, -1)

    wqkv = a["L0_ffn_W_qkv"]
    mats = [quadrants(a["L0_attn_Wq"]), quadrants(a["L0_attn_Wk"]), a["L0_attn_Wv"], a["L0_attn_Wo"],
            quadrants(wqkv[0:D]), wqkv[D:2 * D], wqkv[2 * D:3 * D]]
    arrays = {
        "x": a["x"],
        "xT": a["x"].transpose(0, 2, 1),
        "ctxT": a["ctx_2048"].transpose(0, 2, 1),
        "weights": np.stack([m.T.reshape(CC, P, D) for m in mats]),
        "gate": a["L0_ffn_W_gate"].T,
        "ch_bias": np.stack([quadrants(a["L0_attn_bq"].reshape(D, 1)).reshape(CC, P).T,
                             quadrants(a["L0_attn_bk"].reshape(D, 1)).reshape(CC, P).T,
                             a["L0_attn_bv"].reshape(CC, P).T], axis=1),
        "row_bias": np.broadcast_to(a["L0_attn_bo"], (P, D)),
        "decay": a["L0_xattn_time_decay"].reshape(CC, P).T,
        "first": a["L0_xattn_time_first"].reshape(CC, P).T,
    }
    nc = bacc.Bacc("TRN2", target_bir_lowering=False, num_devices=1)
    fed, args = {}, []
    for name, v in arrays.items():
        v = np.ascontiguousarray(v)
        fed[f"in_{name}"] = v
        args.append(nc.dram_tensor(f"in_{name}", v.shape, mybir.dt.from_np(v.dtype), kind="ExternalInput").ap())
    out = nc.dram_tensor("out_y", (NB, S, D), mybir.dt.float32, kind="ExternalOutput").ap()
    build(nc, *args, out)
    return run(nc, [fed], core_ids=[0]).results[0]["out_y"]
```

```python
import concourse.bass as bass
from concourse import mybir
from contextlib import ExitStack

NB, S, D = 16, 256, 512
NH, HD = 16, 32
P = 128
CC = D // P
TT = S // P
NG = 4
HG = NH // NG
SCALE = float(HD) ** -0.5
EPS = 1e-5
MASKED = -1e30
START_MAX = -1e38

W_Q, W_K, W_V, W_O, W_FQ, W_FK, W_FV = range(7)
NW = 7

PA_JOBS, PA_Q, PA_K, PA_V, PA_WO = 8, 0, 2, 4, 6
PF_JOBS, PF_X2, PF_Q, PF_K, PF_V = 7, 0, 1, 3, 5
A_JOBS, A_M, A_OT = 8, (0, 1, 3, 5), (2, 4, 6, 7)
F_JOBS, F_KT, F_M = 5, 0, (1, 2, 3, 4)
F_LINKS, F_LINK_K3, F_LINK_PICKED = 29, 12, 16
A_LINKS, W_LINKS = 9, 9
TILES = 3 * NG
W_JOBS, W_X1J, W_YJ, W_X2J, W_GATE, W_GATE_T = 7, 0, 2, 4, 5, 6
CONSTS = 2


def build(nc, x_d, xT_d, ctxT_d, weights_d, gate_d, ch_bias_d, row_bias_d, decay_d, first_d, out_d):
    f32, f32r, bf16 = mybir.dt.float32, mybir.dt.float32r, mybir.dt.bfloat16
    ALU, ACT, AX = mybir.AluOpType, mybir.ActivationFunctionType, mybir.AxisListType
    V, A, T, G = nc.vector, nc.scalar, nc.tensor, nc.gpsimd

    ctx = ExitStack()
    with ctx:
        def sb(name, shape, dt=f32):
            return ctx.enter_context(nc.sbuf_tensor(name, shape, dt))

        def overlaid(name, size, *tensors):
            base = nc.sbuf_base
            sb(name, [P, size // 4])
            return [nc.alloc_sbuf_tensor_at(n, shape, dt, offset=base + at) for n, shape, dt, at in tensors]

        def pb(name):
            return ctx.enter_context(nc.psum_tensor(name, [P, 512], f32))

        def sem(name):
            return ctx.enter_context(nc.semaphore(name))

        w_hi = sb("w_hi", [P, NW, CC, D], f32r)
        w_lo = sb("w_lo", [P, NW, CC, D], f32r)
        gate_hi = sb("gate_hi", [P, CC, NH], f32r)
        gate_lo = sb("gate_lo", [P, CC, NH], f32r)
        q_stack = sb("q_stack", [P, NH, S], f32r)
        HC = CC // 2
        behind = NH * S * 4 * (NG - 1) // NG
        k_stack, w_key, w_e1 = overlaid(
            "k_stack_region", NH * S * 4, ("k_stack", [P, NH, S], f32r, 0),
            ("w_key", [P, HC, S], f32, behind), ("w_e1", [P, HC, S], f32, behind + HC * S * 4))
        w_d = sb("w_d", [P, HC, S])
        w_ev = sb("w_ev", [P, HC, S])
        kf_stack, logit_t = overlaid("kf_stack_region", S * 4, ("kf_stack", [P, S], f32r, 0),
                                     ("logit_t", [P, S], f32, 0))
        q_hi, x_raw = overlaid("q_region", CC * S * 4,
                               ("q_hi", [P, CC, S], f32r, 0),
                               ("x_raw", [P, CC, S], f32, 0))
        q_lo = sb("q_lo", [P, CC, S], f32r)
        k_hi = sb("k_hi", [P, CC, S], f32r)
        k_lo = sb("k_lo", [P, CC, S], f32r)
        xt_hi = sb("xt_hi", [P, CC, S], f32r)
        xt_lo = sb("xt_lo", [P, CC, S], f32r)
        xa = sb("xa", [P, TT, D])
        xb = sb("xb", [P, TT, D])
        v_a = sb("v_a", [P, TT, NH, HD + 1])
        v_f = sb("v_f", [P, TT, HD + 1])
        prob0 = sb("prob0", [P, HG, S])
        prob1 = sb("prob1", [P, HG, P])
        o_tok = sb("o_tok", [P, TT, HG * HD])
        bo_row = sb("bo_row", [P, D])
        ch_bias = sb("ch_bias", [P, 3, CC])
        neg_max = sb("neg_max", [P, HG, TT])
        neg_parts = sb("neg_parts", [P, 2, HG, TT], f32r)
        max_rows = sb("max_rows", [2 * HG * TT, P], f32r)
        ident = sb("ident", [P, P])
        ident_b = sb("ident_b", [P, P], bf16)
        mask_qk = sb("mask_qk", [P, P], bf16)
        mask_kq = sb("mask_kq", [P, P], bf16)
        o_rec = sb("o_rec", [P, TT * HG])
        w_val = sb("w_val", [P, HC, S])
        picked = w_val[:].rearrange("p c t -> p (c t)").rearrange("p (h d) -> p h d", h=NH)
        w_max = sb("w_max", [P, HC, S + 1])
        w_e2 = sb("w_e2", [P, HC, S + 1])
        w_y = sb("w_y", [P, HC, S])
        decay = sb("decay", [P, CC])
        first = sb("first", [P, CC])
        stats = sb("stats", [P, 3, TT, 6])
        spare = sb("spare", [P, 3])
        spare_pool = sb("spare_pool", [P, 1])
        eps = sb("eps", [P, TT])
        meanvar = sb("meanvar", [P, 3, TT, 2])
        var_eps = sb("var_eps", [P, 3, TT])
        rstd = sb("rstd", [P, 3, TT])
        minus_half = sb("minus_half", [P, TT])
        logit = sb("logit", [P, TT, NH])
        g_max = sb("g_max", [P, TT])
        g_nmax = sb("g_nmax", [P, TT])
        g_eq = sb("g_eq", [P, TT, NH])
        g_rank = sb("g_rank", [P, TT, NH])
        g_top = sb("g_top", [P, TT])
        g_ind = sb("g_ind", [P, TT, NH])
        g_exp = sb("g_exp", [P, TT, NH])
        g_sum = sb("g_sum", [P, TT])
        g_val = sb("g_val", [P, TT])
        rank = sb("rank", [P, NH])
        k_sel = sb("k_sel", [P, TT, HD])
        v_sel = sb("v_sel", [P, TT, HD])
        gate = k_sel[:].rearrange("p c d -> p (c d)").rearrange("p (c h) -> p c h", c=CC)
        k3 = sb("k3", [P, TT, 3, HD], f32r)

        pp = pb("pp")
        pt = pb("pt")
        sq = [pb("sq0"), pb("sq1")]
        sk = [pb("sk0"), pb("sk1")]
        po = pb("po")
        pw = pb("pw")

        load_w = [sem(f"load_w{i}") for i in range(4)]
        load_c, load_xr, load_xa = sem("load_c"), sem("load_xr"), sem("load_xa")
        load_v = [sem(f"load_v{i}") for i in range(2)]
        w_split_hi, w_split_lo = sem("w_split_hi"), sem("w_split_lo")
        consts, zero_done = sem("consts"), sem("zero_done")
        xt_hi_ready, xt_ready, xa_ready = sem("xt_hi_ready"), sem("xt_ready"), sem("xa_ready")
        a_job, a_free, f_job, f_free = sem("a_job"), sem("a_free"), sem("f_job"), sem("f_free")
        pa_job, pa_free, pf_job, pf_free = sem("pa_job"), sem("pa_free"), sem("pf_job"), sem("pf_free")
        pa_hi, pf_hi, ot_hi, x2_hi = sem("pa_hi"), sem("pf_hi"), sem("ot_hi"), sem("x2_hi")
        a_sq, a_max, f_sq, f_max = sem("a_sq"), sem("a_max"), sem("f_sq"), sem("f_max")
        a_neg, f_neg = sem("a_neg"), sem("f_neg")
        a_sk, a_exp, f_sk, f_exp = sem("a_sk"), sem("a_exp"), sem("f_sk"), sem("f_exp")
        a_po, a_norm, f_po, f_norm = sem("a_po"), sem("a_norm"), sem("f_po"), sem("f_norm")
        a_stk = [sem(f"a_stk{g}") for g in range(NG)]
        f_stk = [sem(f"f_stk{g}") for g in range(NG)]
        a_mrow = [sem(f"a_mrow{g}") for g in range(NG)]
        f_mrow = [sem(f"f_mrow{g}") for g in range(NG)]
        w_job, w_free = sem("w_job"), sem("w_free")
        w_pp, w_diff, w_even, w_min = sem("w_pp"), sem("w_diff"), sem("w_even"), sem("w_min")
        w_carry, w_now, w_evr, w_scan = sem("w_carry"), sem("w_now"), sem("w_evr"), sem("w_scan")
        w_den, w_rec, w_yr, w_ones = sem("w_den"), sem("w_rec"), sem("w_yr"), sem("w_ones")
        ln_stat = [sem(f"ln_stat{n}") for n in range(3)]
        ln_rstd = [sem(f"ln_rstd{n}") for n in range(3)]
        x1_ready, x2_ready, x3_ready = sem("x1_ready"), sem("x2_ready"), sem("x3_ready")
        g_ready, g_summed = sem("g_ready"), sem("g_summed")
        stored = sem("stored")
        dve_a, dve_w, dve_f, dve_once = sem("dve_a"), sem("dve_w"), sem("dve_f"), sem("dve_once")
        pool_w, pool_once, act_once = sem("pool_w"), sem("pool_once"), sem("act_once")
        pool_ln = [sem(f"pool_ln{n}") for n in range(3)]

        def slot(n):
            if n % 4 < 2:
                return xb[:, n % 4, :]
            return (w_y, w_ev)[n % 2][:].rearrange("p c t -> p (c t)")

        def wait(eng, s, value):
            if not isinstance(value, int) or value > 0:
                eng.wait_ge(s, value)

        class Chain:
            def __init__(self, eng, s, per, b):
                self.eng, self.s, self.base, self.per, self.n = eng, s, per * b, per, 0

            def mark(self, ins):
                ins.then_inc(self.s, 1)
                self.n += 1

            def wait(self):
                self.eng.wait_ge(self.s, self.base + self.n)

            def link(self, ins):
                self.mark(ins)
                self.wait()

            def close(self):
                assert self.n == self.per, self.n

        def values_done(b):
            return PA_JOBS * NB if isinstance(b, int) and b == NB else PA_JOBS * b + PA_WO

        block = ctx.enter_context(nc.Block())

        @block.sync
        def _(sp):
            def load_xr_of(b, stk, count):
                for g in range(NG):
                    wait(sp, stk[g], count)
                sp.dma_start(x_raw[:], xT_d[b].rearrange("(c p) t -> p c t", p=P)).then_inc(load_xr, 16)

            def stack(dst, lo, src, g, s):
                sp.dma_start(dst[lo:lo + HD, HG * g:HG * (g + 1), :].bitcast(f32),
                             src[HD * g:HD * (g + 1), :, :].bitcast(f32)).then_inc(s, 16)

            def stack_max(b, g, job, jobs, s_free, mrow):
                wait(sp, s_free, jobs * b + job[g] + 1)
                sp.dma_start(q_stack[3 * HD:3 * HD + 2, HG * g:HG * (g + 1), :].bitcast(f32),
                             max_rows[:].bitcast(f32)).then_inc(mrow[g], 16)

            def load_ctx(b, c):
                if c >= HC:
                    wait(sp, w_den, 2 * (CC * b + c - HC + 1))
                sp.dma_start(w_val[:, c % HC, :], ctxT_d[b, P * c:P * (c + 1)]).then_inc(load_v[c % HC], 16)

            def store(b):
                wait(sp, x3_ready, b + 1)
                sp.dma_start(out_d[b].rearrange("(c p) d -> p c d", p=P), xb[:]).then_inc(stored, 16)

            def q_stacks(b, jobs, job, s_free, groups, s_used, used, stk):
                if jobs is not None:
                    wait(sp, s_free, jobs * b + job + 2)
                for g in groups:
                    if s_used is not None:
                        wait(sp, s_used, used + 3 * (g + 1))
                    for lo, src in ((0, q_hi), (HD, q_hi), (2 * HD, q_lo)):
                        stack(q_stack, lo, src, g, stk[g])

            def k_stacks(b, groups):
                if groups[0] == 0:
                    wait(sp, pa_free, PA_JOBS * b + PA_K + 2)
                if groups[0] == NG - 1:
                    wait(sp, w_ones, b + 1)
                for g in groups:
                    for lo, src in ((0, k_hi), (HD, k_lo), (2 * HD, k_hi)):
                        stack(k_stack, lo, src, g, a_stk[g])

            def load_weights(*which):
                for w in which:
                    for n in range(CC * w, CC * (w + 1)):
                        wait(sp, w_split_lo, n - 3)
                        sp.dma_start(slot(n), weights_d[w, n % CC]).then_inc(load_w[n % 4], 16)

            def max_a(b, g):
                stack_max(b, g, A_M, A_JOBS, a_free, a_mrow)

            def max_f(b, g):
                stack_max(b, g, F_M, F_JOBS, f_free, f_mrow)

            def iteration(t, do_a, prev, nxt):
                b = t - 1
                if do_a:
                    max_a(t, 1)
                    if not prev:
                        load_weights(W_FQ)
                    k_stacks(t, range(NG - 1, NG))
                if prev and not (isinstance(t, int) and t < 2):
                    store(t - 2)
                if do_a:
                    max_a(t, 2)
                    if not prev:
                        load_weights(W_FK)
                    wait(sp, x2_ready, t)
                    sp.dma_start(xa[:], x_d[t].rearrange("(c p) d -> p c d", p=P)).then_inc(load_xa, 16)
                if prev:
                    q_stacks(b, PF_JOBS, PF_Q, pf_free, range(NG - 1), a_sk if do_a else None, TILES * t, f_stk)
                if do_a:
                    max_a(t, 3)
                    if not prev:
                        load_weights(W_FV)
                if prev:
                    q_stacks(b, None, None, None, range(NG - 1, NG), a_sk if do_a else None, TILES * t, f_stk)
                if nxt:
                    if prev:
                        load_xr_of(t + 1, f_stk, 48 * t)
                    else:
                        load_xr_of(t + 1, a_stk, 96 * (t + 1))
                if prev:
                    max_f(b, 0)
                    if do_a:
                        wait(sp, dve_f, F_LINKS * b + F_LINK_PICKED)
                if do_a:
                    load_ctx(t, 0)
                    load_ctx(t, 1)
                if prev:
                    max_f(b, 1)
                    max_f(b, 2)
                if nxt:
                    q_stacks(t + 1, PA_JOBS, PA_Q, pa_free, range(NG - 2), f_sk if prev else None, TILES * b, a_stk)
                if prev:
                    max_f(b, 3)
                if nxt:
                    k_stacks(t + 1, range(1))
                if do_a:
                    load_ctx(t, 2)
                    load_ctx(t, 3)
                if nxt:
                    q_stacks(t + 1, None, None, None, range(NG - 2, NG), f_sk if prev else None, TILES * b, a_stk)
                    k_stacks(t + 1, range(1, 2))
                    max_a(t + 1, 0)
                    k_stacks(t + 1, range(2, 3))

            sp.dma_start(ch_bias[:], ch_bias_d).then_inc(load_c, 16)
            sp.dma_start(decay[:], decay_d).then_inc(load_c, 16)
            sp.dma_start(first[:], first_d).then_inc(load_c, 16)
            sp.dma_start(bo_row[:], row_bias_d).then_inc(load_c, 16)
            sp.dma_start(gate, gate_d.rearrange("(c p) h -> p c h", p=P)).then_inc(load_c, 16)
            load_xr_of(0, a_stk, 0)
            load_weights(W_Q, W_K, W_V)
            q_stacks(0, PA_JOBS, PA_Q, pa_free, range(NG), None, 0, a_stk)
            k_stacks(0, range(NG - 1))
            load_weights(W_O)
            max_a(0, 0)
            iteration(0, True, False, True)
            iteration(1, True, True, True)
            with sp.Fori(2, NB - 1) as t:
                iteration(t, True, True, True)
            iteration(NB - 1, True, True, False)
            iteration(NB, False, True, False)
            store(NB - 1)
            sp.wait_ge(stored, 16 * NB)

        @block.tensor
        def _(pe):
            def products(out, lhs, rhs):
                for c in range(CC):
                    (lh, ll), (rh, rl) = lhs(c), rhs(c)
                    T.matmul(out, lh, rh, start=(c == 0), stop=False, skip_group_check=True)
                    T.matmul(out, lh, rl, start=False, stop=False, skip_group_check=True)
                    mm = T.matmul(out, ll, rh, start=False, stop=(c == CC - 1), skip_group_check=True)
                return mm

            def weight(w, lo, n):
                return lambda c: (w_hi[:, w, c, lo:lo + n], w_lo[:, w, c, lo:lo + n])

            def tokens(lo, n, hi_t=xt_hi, lo_t=xt_lo):
                return lambda c: (hi_t[:, c, lo:lo + n], lo_t[:, c, lo:lo + n])

            def channels_out(w, pair):
                for i in range(2):
                    mm = products(pp[:, S * i:S * (i + 1)], weight(w, P * (2 * pair + i), P), tokens(0, S))
                return mm

            def tokens_out(bank, w, c, hi_t=xt_hi, lo_t=xt_lo):
                return products(bank[:, 0:D], tokens(P * c, P, hi_t, lo_t), weight(w, 0, D))

            def scores_sq(b, g, tiles, stk, per, key, s_sq, s_max):
                if tiles[0] == 0:
                    pe.wait_ge(stk[g], per * (b + 1))
                for i in tiles:
                    n = 3 * g + i
                    if n >= 2:
                        pe.wait_ge(s_max, TILES * b + n - 1)
                    out = sq[n % 2]
                    if i == 0:
                        for k in range(HG):
                            h = HG * g + k
                            T.matmul(out[:, P * k:P * (k + 1)], q_stack[0:3 * HD, h, 0:P], key(h, 0, P, 3 * HD),
                                     start=(k == 0), stop=False, skip_group_check=True)
                        for k in range(HG):
                            mm = T.matmul(out[:, P * k:P * (k + 1)], ident_b[:], mask_qk[:],
                                          start=False, stop=(k == HG - 1), skip_group_check=True)
                    else:
                        for k in range(2):
                            h = HG * g + 2 * (i - 1) + k
                            T.matmul(out[:, S * k:S * (k + 1)], q_stack[0:3 * HD, h, P:S], key(h, 0, S, 3 * HD),
                                     start=(k == 0), stop=False, skip_group_check=True)
                        for k in range(2):
                            mm = T.matmul(out[:, S * k + P:S * (k + 1)], ident_b[:], mask_qk[:],
                                          start=False, stop=(k == 1), skip_group_check=True)
                    mm.then_inc(s_sq, 1)

            def max_transpose(s_neg, count, s_before, before, s_job):
                pe.wait_ge(s_neg, count)
                wait(pe, s_before, before)
                T.transpose(pt[0:2 * HG * TT, 0:P], neg_parts[:].rearrange("p a h c -> p (a h c)").bitcast(f32),
                            ident[:]).then_inc(s_job, 1)

            def scores_sk(b, g, tiles, mrow, key, s_sk, s_exp):
                if tiles[0] == 0:
                    pe.wait_ge(mrow[g], 16 * (b + 1))
                rows = 3 * HD + 2
                for i in tiles:
                    n = 3 * g + i
                    if n >= 2:
                        pe.wait_ge(s_exp, TILES * b + n - 1)
                    out = sk[n % 2]
                    if i < 2:
                        for k in range(2):
                            h = HG * g + 2 * i + k
                            T.matmul(out[:, S * k:S * (k + 1)], key(h, 0, P, rows), q_stack[0:rows, h, :],
                                     start=(k == 0), stop=False, skip_group_check=True)
                        for k in range(2):
                            mm = T.matmul(out[:, S * k:S * k + P], ident_b[:], mask_kq[:],
                                          start=False, stop=(k == 1), skip_group_check=True)
                    else:
                        for k in range(HG):
                            h = HG * g + k
                            T.matmul(out[:, P * k:P * (k + 1)], key(h, P, P, rows), q_stack[0:rows, h, P:S],
                                     start=(k == 0), stop=False, skip_group_check=True)
                        for k in range(HG):
                            mm = T.matmul(out[:, P * k:P * (k + 1)], ident_b[:], mask_kq[:],
                                          start=False, stop=(k == HG - 1), skip_group_check=True)
                    mm.then_inc(s_sk, 1)

            def values(b, g, value, s_exp, s_norm, s_po):
                if g:
                    pe.wait_ge(s_norm, NG * b + g)
                pe.wait_ge(s_exp, TILES * b + 3 * (g + 1))
                out = po[:, 0:TT * HG * (HD + 1)].rearrange("p (c h d) -> p c h d", c=TT, h=HG)
                for k in range(HG):
                    h = HG * g + k
                    T.matmul(out[:, 0, k, :], prob0[:, k, 0:P], value(0, h),
                             start=True, stop=True, skip_group_check=True)
                    T.matmul(out[:, 1, k, :], prob0[:, k, P:S], value(0, h),
                             start=True, stop=False, skip_group_check=True)
                    mm = T.matmul(out[:, 1, k, :], prob1[:, k, :], value(1, h),
                                  start=False, stop=True, skip_group_check=True)
                mm.then_inc(s_po, 1)

            def out_transpose(b, g, s_before, before):
                pe.wait_ge(a_norm, NG * b + g + 1)
                wait(pe, s_before, before)
                for c in range(TT):
                    mm = T.transpose(pt[:, P * c:P * (c + 1)], o_tok[:, c, :], ident[:])
                mm.then_inc(a_job, 1)

            def turn_half(bank, src, half):
                for i in range(HC):
                    for c in range(TT):
                        ch = P * (HC * half + i)
                        mm = T.transpose(bank[:, S * i + P * c:S * i + P * (c + 1)], src[:, c, ch:ch + P], ident[:])
                return mm

            def x1_transpose(b, half):
                pe.wait_ge(x1_ready, b + 1)
                wait(pe, w_free, W_JOBS * b + W_X1J + half)
                turn_half(pw, xa, half).then_inc(w_job, 1)

            def x2_transpose(b):
                pe.wait_ge(x2_ready, b + 1)
                pe.wait_ge(w_free, W_JOBS * b + W_X2J)
                turn_half(pw, xb, 0).then_inc(w_job, 1)
                pe.wait_ge(pa_free, values_done(b + 1))
                turn_half(pp, xb, 1).then_inc(pf_job, 1)

            def y_transpose(b, half):
                pe.wait_ge(w_yr, CC * b + HC * (half + 1))
                pe.wait_ge(w_free, W_JOBS * b + W_YJ + half)
                for c in range(TT):
                    for i in range(HC):
                        at = HC * P * c + P * i
                        mm = T.transpose(pw[:, at:at + P], w_y[:, i, P * c:P * (c + 1)], ident[:])
                mm.then_inc(w_job, 1)

            def key_a(h, lo, n, rows):
                return k_stack[0:rows, h, lo:lo + n]

            def key_f(h, lo, n, rows):
                return kf_stack[0:rows, lo:lo + n]

            def weight_split(b, w):
                if isinstance(b, int) and b == 0:
                    pe.wait_ge(w_split_lo, CC * (w + 1))

            def project_a(b, job):
                weight_split(b, (W_Q, W_K, W_V, W_O)[job // 2])
                if job == PA_Q:
                    pe.wait_ge(xt_ready, b + 1)
                if job == PA_WO:
                    wait(pe, pf_free, PF_JOBS * b)
                    pe.wait_ge(a_free, A_JOBS * (b + 1))
                if job != PA_WO:
                    wait(pe, pa_free, PA_JOBS * b + job)
                if job < PA_K:
                    mm = channels_out(W_Q, job - PA_Q)
                elif job < PA_V:
                    mm = channels_out(W_K, job - PA_K)
                elif job < PA_WO:
                    mm = tokens_out(pp, W_V, job - PA_V)
                else:
                    mm = tokens_out(pp, W_O, job - PA_WO, k_hi, k_lo)
                mm.then_inc(pa_job, 1)

            def project_f(b, job):
                if job == PF_Q:
                    pe.wait_ge(w_free, W_JOBS * b + W_X2J + 1)
                weight_split(b, W_FQ if job < PF_K else W_FK if job < PF_V else W_FV)
                pe.wait_ge(pf_free, PF_JOBS * b + job)
                if job < PF_K:
                    mm = channels_out(W_FQ, job - PF_Q)
                elif job < PF_V:
                    mm = tokens_out(pp, W_FK, job - PF_K)
                else:
                    mm = tokens_out(pp, W_FV, job - PF_V)
                mm.then_inc(pf_job, 1)

            def key_transpose(b, s_before, before):
                pe.wait_ge(dve_f, F_LINKS * b + F_LINK_K3)
                wait(pe, s_before, before)
                for c in range(TT):
                    mm = T.transpose(pt[0:3 * HD, P * c:P * (c + 1)],
                                     k3[:, c, :, :].rearrange("p a d -> p (a d)").bitcast(f32), ident[:])
                mm.then_inc(f_job, 1)

            def gate_logits(b):
                pe.wait_ge(w_free, W_JOBS * b + W_GATE)
                products(pw[0:NH, 0:S], lambda c: (gate_hi[:, c, :], gate_lo[:, c, :]), tokens(0, S)).then_inc(w_job, 1)

            def gate_transpose(b):
                pe.wait_ge(w_free, W_JOBS * b + W_GATE_T)
                for c in range(TT):
                    mm = T.transpose(pw[:, P * c:P * (c + 1)], logit_t[:, P * c:P * (c + 1)], ident[:])
                mm.then_inc(w_job, 1)

            def sq_a(b, g, *tiles):
                scores_sq(b, g, tiles, a_stk, 96, key_a, a_sq, a_max)

            def sq_f(b, g, *tiles):
                scores_sq(b, g, tiles, f_stk, 48, key_f, f_sq, f_max)

            def sk_a(b, g, *tiles):
                scores_sk(b, g, tiles, a_mrow, key_a, a_sk, a_exp)

            def sk_f(b, g, *tiles):
                scores_sk(b, g, tiles, f_mrow, key_f, f_sk, f_exp)

            def max_a(b, g, s_before=None, before=0):
                if s_before is None:
                    s_before, before = a_free, A_JOBS * b + A_M[g]
                max_transpose(a_neg, NG * b + g + 1, s_before, before, a_job)

            def max_f(b, g, s_before=None, before=0):
                if s_before is None:
                    s_before, before = f_free, F_JOBS * b + F_M[g]
                max_transpose(f_neg, NG * b + g + 1, s_before, before, f_job)

            def values_a(b, g):
                values(b, g, value_a, a_exp, a_norm, a_po)

            def values_f(b, g):
                values(b, g, value_f, f_exp, f_norm, f_po)

            def iteration(t, do_a, prev, nxt):
                b = t - 1
                a_done = t + 1 if do_a else NB
                if do_a:
                    sq_a(t, 1, 0, 1)
                    sk_a(t, 0, 2)
                    sq_a(t, 1, 2)
                    project_a(t, PA_V + 1)
                    max_a(t, 1)
                    pe.wait_ge(pa_free, values_done(t))
                    wait(pe, f_norm, NG * b)
                    wait(pe, a_norm, NG * t)
                    values_a(t, 0)
                if prev:
                    y_transpose(b, 1)
                if do_a:
                    sk_a(t, 1, 0, 1)
                    sq_a(t, 2, 0, 1)
                    sk_a(t, 1, 2)
                    out_transpose(t, 0, a_free, A_JOBS * t + A_OT[0])
                    sq_a(t, 2, 2)
                if prev:
                    x2_transpose(b)
                if do_a:
                    values_a(t, 1)
                    max_a(t, 2)
                if prev:
                    project_f(b, PF_Q)
                if do_a:
                    sk_a(t, 2, 0, 1)
                    sq_a(t, 3, 0, 1)
                    sk_a(t, 2, 2)
                    out_transpose(t, 1, a_free, A_JOBS * t + A_OT[1])
                if prev:
                    project_f(b, PF_Q + 1)
                if do_a:
                    sq_a(t, 3, 2)
                if prev:
                    gate_logits(b)
                    project_f(b, PF_K)
                    gate_transpose(b)
                if do_a:
                    max_a(t, 3)
                    values_a(t, 2)
                if prev:
                    project_f(b, PF_K + 1)
                if do_a:
                    sk_a(t, 3, 0, 1)
                    out_transpose(t, 2, a_free, A_JOBS * t + A_OT[2])
                if prev:
                    project_f(b, PF_V)
                    key_transpose(b, a_free, A_JOBS * t + A_OT[2] + 1 if do_a else A_JOBS * NB)
                if do_a:
                    sk_a(t, 3, 2)
                if prev:
                    pe.wait_ge(f_free, F_JOBS * b + F_KT + 1)
                    wait(pe, a_max, TILES * a_done)
                    sq_f(b, 0, 0, 1, 2)
                if do_a:
                    values_a(t, 3)
                if prev:
                    max_f(b, 0)
                    project_f(b, PF_V + 1)
                    wait(pe, a_exp, TILES * a_done)
                    sk_f(b, 0, 0, 1)
                    sq_f(b, 1, 0, 1)
                    sk_f(b, 0, 2)
                if do_a:
                    if prev:
                        wait(pe, f_free, F_JOBS * b + F_M[0] + 1)
                    out_transpose(t, 3, a_free, A_JOBS * t + A_OT[3])
                if prev:
                    sq_f(b, 1, 2)
                    wait(pe, a_norm, NG * a_done)
                    pe.wait_ge(dve_f, F_LINKS * b + F_LINK_PICKED + 1)
                    if not do_a:
                        max_f(b, 1, a_free, A_JOBS * a_done)
                    values_f(b, 0)
                    if do_a:
                        max_f(b, 1, a_free, A_JOBS * a_done)
                if do_a:
                    project_a(t, PA_WO)
                if prev:
                    sk_f(b, 1, 0, 1)
                if do_a:
                    project_a(t, PA_WO + 1)
                if prev:
                    sq_f(b, 2, 0, 1)
                    sk_f(b, 1, 2)
                if nxt:
                    project_a(t + 1, PA_Q)
                if prev:
                    sq_f(b, 2, 2)
                if do_a:
                    x1_transpose(t, 0)
                if prev:
                    if not nxt:
                        max_f(b, 2)
                    values_f(b, 1)
                    if nxt:
                        max_f(b, 2)
                if nxt:
                    project_a(t + 1, PA_Q + 1)
                if prev:
                    sk_f(b, 2, 0, 1)
                    sq_f(b, 3, 0, 1)
                    sk_f(b, 2, 2)
                if nxt:
                    project_a(t + 1, PA_K)
                if prev:
                    sq_f(b, 3, 2)
                if do_a:
                    x1_transpose(t, 1)
                if prev:
                    if not nxt:
                        max_f(b, 3)
                    values_f(b, 2)
                    if nxt:
                        max_f(b, 3)
                if nxt:
                    project_a(t + 1, PA_K + 1)
                if prev:
                    sk_f(b, 3, 0, 1)
                    sk_f(b, 3, 2)
                    values_f(b, 3)
                if nxt:
                    wait(pe, f_max, TILES * t)
                    wait(pe, a_max, TILES * (t + 1))
                    sq_a(t + 1, 0, 0, 1, 2)
                if do_a:
                    y_transpose(t, 0)
                if nxt:
                    if prev:
                        max_a(t + 1, 0, f_free, F_JOBS * t)
                        pe.wait_ge(f_exp, TILES * t)
                    else:
                        max_a(t + 1, 0)
                        wait(pe, a_exp, TILES * (t + 1))
                    project_a(t + 1, PA_V)
                    sk_a(t + 1, 0, 0, 1)

            def value_a(c, h):
                return v_a[:, c, h, :]

            def value_f(c, h):
                return v_f[:, c, :]

            pe.wait_ge(consts, CONSTS)
            for job in range(PA_V + 1):
                project_a(0, job)
            sq_a(0, 0, 0, 1, 2)
            max_a(0, 0)
            sk_a(0, 0, 0, 1)
            iteration(0, True, False, True)
            iteration(1, True, True, True)
            with pe.Fori(2, NB - 1) as t:
                iteration(t, True, True, True)
            iteration(NB - 1, True, True, False)
            iteration(NB, False, True, False)

        @block.scalar
        def _(act):
            def split_hi(*which):
                for w in which:
                    for n in range(CC * w, CC * (w + 1)):
                        act.wait_ge(load_w[n % 4], 16 * (n // 4 + 1))
                        A.activation(w_hi[:, w, n % CC, :], slot(n), ACT.Copy).then_inc(w_split_hi, 1)

            def exps(b, g, tiles, s_sk, s_exp):
                for i in tiles:
                    n = 3 * g + i
                    act.wait_ge(s_sk, TILES * b + n + 1)
                    if i < 2:
                        dst = prob0[:, 2 * i:2 * i + 2, :].rearrange("p h q -> p (h q)")
                    else:
                        dst = prob1[:].rearrange("p h q -> p (h q)")
                    A.activation(dst, sk[n % 2][:], ACT.Exp, scale=SCALE).then_inc(s_exp, 1)

            def exps_a(b, g, *tiles):
                exps(b, g, tiles, a_sk, a_exp)

            def exps_f(b, g, *tiles):
                exps(b, g, tiles, f_sk, f_exp)

            def out_hi(b, g):
                act.wait_ge(a_job, A_JOBS * b + A_OT[g] + 1)
                if g == 0:
                    for stk in a_stk:
                        act.wait_ge(stk, 96 * (b + 1))
                A.activation(k_hi[:, g, :], pt[:, 0:S], ACT.Identity, bias=ch_bias[:, 2, g:g + 1])\
                    .then_inc(ot_hi, 1)

            def carry_exps(b, c):
                act.wait_ge(w_diff, CC * b + c + 1)
                A.activation(w_e1[:, c % HC, :], w_e1[:, c % HC, :], ACT.Exp, bias=decay[:, c:c + 1])
                if c % HC == 0:
                    act.wait_ge(w_even, HC * b + c // HC + 1)
                else:
                    act.wait_ge(w_free, W_JOBS * b + W_X1J + c // HC + 1)
                A.activation(w_e2[:, c % HC, 1:S + 1], w_e2[:, c % HC, 1:S + 1], ACT.Exp).then_inc(w_carry, 1)

            def now_exps(b, c):
                act.wait_ge(w_min, CC * b + c + 1)
                A.activation(w_key[:, c % HC, :], w_key[:, c % HC, :], ACT.Exp)
                A.activation(w_d[:, c % HC, :], w_d[:, c % HC, :], ACT.Exp).then_inc(w_now, 1)

            def x_split_hi(b):
                act.wait_ge(load_xr, 16 * (b + 1))
                wait(act, pf_job, PF_JOBS * (b - 1))
                wait(act, pa_job, PA_JOBS * (b - 1) + PA_WO)
                A.activation(xt_hi[:], x_raw[:], ACT.Copy).then_inc(xt_hi_ready, 1)

            def qk_hi(b, job):
                which, n = (0, job - PA_Q) if job < PA_K else (1, job - PA_K)
                dst = (q_hi, k_hi)[which]
                act.wait_ge(pa_job, PA_JOBS * b + job + 1)
                for i in range(2):
                    c = 2 * n + i
                    e = A.activation(dst[:, c, :], pp[:, S * i:S * (i + 1)], ACT.Identity,
                                     bias=ch_bias[:, which, c:c + 1])
                e.then_inc(pa_hi, 1)

            def value_out(b, c):
                act.wait_ge(pa_job, PA_JOBS * b + PA_V + c + 1)
                A.activation(v_a[:, c, :, 0:HD], pp[:].rearrange("p (h d) -> p h d", h=NH), ACT.Copy)\
                    .then_inc(pa_free, 1)

            def fq_hi(b, n):
                act.wait_ge(pf_job, PF_JOBS * b + PF_Q + n + 1)
                A.activation(q_hi[:, 2 * n:2 * n + 2, :].rearrange("p c t -> p (c t)"), pp[:], ACT.Copy)\
                    .then_inc(pf_hi, 1)

            def gate_sums(b):
                act.wait_ge(g_ready, b + 1)
                for c in range(TT):
                    e = A.activation(g_exp[:, c, :], logit[:, c, :], ACT.Exp, bias=g_nmax[:, c:c + 1],
                                     accum_out=g_sum[:, c:c + 1])
                e.then_inc(g_summed, 1)

            def iteration(t, do_a, prev, nxt):
                b = t - 1
                if do_a:
                    exps_a(t, 0, 2)
                    value_out(t, 1)
                    exps_a(t, 1, 0, 1)
                    if not prev:
                        split_hi(W_O)
                    exps_a(t, 1, 2)
                    out_hi(t, 0)
                if prev:
                    x2_split_hi(b)
                if do_a:
                    exps_a(t, 2, 0, 1)
                    if not prev:
                        split_hi(W_FQ)
                if prev:
                    fq_hi(b, 0)
                if do_a:
                    exps_a(t, 2, 2)
                    out_hi(t, 1)
                if prev:
                    fq_hi(b, 1)
                    gate_sums(b)
                if do_a:
                    exps_a(t, 3, 0, 1)
                    if not prev:
                        split_hi(W_FK)
                    out_hi(t, 2)
                    exps_a(t, 3, 2)
                    if not prev:
                        split_hi(W_FV)
                if prev:
                    exps_f(b, 0, 0, 1)
                    exps_f(b, 0, 2)
                if nxt:
                    x_split_hi(t + 1)
                if do_a:
                    out_hi(t, 3)
                if prev:
                    exps_f(b, 1, 0, 1)
                    exps_f(b, 1, 2)
                if nxt:
                    qk_hi(t + 1, PA_Q)
                    qk_hi(t + 1, PA_Q + 1)
                if do_a:
                    carry_exps(t, 0)
                if prev:
                    exps_f(b, 2, 0, 1)
                if do_a:
                    carry_exps(t, 1)
                    now_exps(t, 0)
                if prev:
                    exps_f(b, 2, 2)
                if do_a:
                    now_exps(t, 1)
                if nxt:
                    qk_hi(t + 1, PA_K)
                    qk_hi(t + 1, PA_K + 1)
                if prev:
                    exps_f(b, 3, 0, 1)
                    exps_f(b, 3, 2)
                if do_a:
                    carry_exps(t, 2)
                    now_exps(t, 2)
                    carry_exps(t, 3)
                    now_exps(t, 3)
                if nxt:
                    value_out(t + 1, 0)
                    exps_a(t + 1, 0, 0, 1)

            def x2_split_hi(b):
                for half, s_job, count, bank in ((0, w_job, W_JOBS * b + W_X2J + 1, pw),
                                                 (1, pf_job, PF_JOBS * b + PF_X2 + 1, pp)):
                    act.wait_ge(s_job, count)
                    A.activation(xt_hi[:, HC * half:HC * (half + 1), :].rearrange("p c t -> p (c t)"), bank[:],
                                 ACT.Copy).then_inc(x2_hi, 1)

            act.wait_ge(load_c, 16 * 5)
            A.activation(gate_hi[:], gate, ACT.Copy).then_inc(w_split_hi, 1)
            A.activation(decay[:], decay[:], ACT.Exp).then_inc(act_once, 1)
            act.wait_ge(act_once, 1)
            A.activation(decay[:], decay[:], ACT.Copy, scale=-1.0).then_inc(act_once, 1)
            act.wait_ge(act_once, 2)
            x_split_hi(0)
            split_hi(W_Q, W_K)
            for job in range(PA_V):
                qk_hi(0, job)
            split_hi(W_V)
            value_out(0, 0)
            exps_a(0, 0, 0, 1)
            iteration(0, True, False, True)
            iteration(1, True, True, True)
            with act.Fori(2, NB - 1) as t:
                iteration(t, True, True, True)
            iteration(NB - 1, True, True, False)
            iteration(NB, False, True, False)

        @block.vector
        def _(dve):
            def split_lo(*which):
                for w in which:
                    for n in range(CC * w, CC * (w + 1)):
                        dve.wait_ge(w_split_hi, n + 2)
                        V.tensor_tensor(w_lo[:, w, n % CC, :], slot(n), w_hi[:, w, n % CC, :].bitcast(f32),
                                        ALU.subtract).then_inc(w_split_lo, 1)

            def maxima(ch, b, g, tiles, s_sq, s_max, s_neg):
                for i in tiles:
                    n = 3 * g + i
                    dve.wait_ge(s_sq, TILES * b + n + 1)
                    if i == 0:
                        src, dst = sq[n % 2][:].rearrange("p (h k) -> p h k", h=HG), neg_max[:, :, 0]
                    else:
                        src = sq[n % 2][:].rearrange("p (h k) -> p h k", h=2)
                        dst = neg_max[:, 2 * (i - 1):2 * i, 1]
                    V.tensor_reduce(dst, src, AX.X, ALU.max, negate=True).then_inc(s_max, 1)
                if tiles[-1] != 2:
                    return
                dve.wait_ge(s_max, TILES * b + 3 * (g + 1))
                ch.link(V.tensor_copy(neg_parts[:, 0, :, :], neg_max[:]))
                V.tensor_tensor(neg_parts[:, 1, :, :], neg_max[:], neg_parts[:, 0, :, :].bitcast(f32),
                                ALU.subtract).then_inc(s_neg, 1)

            def rows(b, g, job, jobs, s_job, s_free, s_read, read):
                dve.wait_ge(s_job, jobs * b + job[g] + 1)
                wait(dve, s_read, read)
                V.tensor_copy(max_rows[:], pt[0:2 * HG * TT, 0:P]).then_inc(s_free, 1)

            def maxima_a(ch, b, g, *tiles):
                maxima(ch, b, g, tiles or (0, 1, 2), a_sq, a_max, a_neg)

            def maxima_f(ch, b, g, *tiles):
                maxima(ch, b, g, tiles or (0, 1, 2), f_sq, f_max, f_neg)

            def rows_a(b, g, s_read=None, read=0):
                if g:
                    s_read, read = a_mrow[g - 1], 16 * (b + 1)
                rows(b, g, A_M, A_JOBS, a_job, a_free, s_read, read)

            def rows_f(b, g, s_read=None, read=0):
                if g:
                    s_read, read = f_mrow[g - 1], 16 * (b + 1)
                rows(b, g, F_M, F_JOBS, f_job, f_free, s_read, read)

            def normalise(ch, b, g, s_po, s_norm):
                dve.wait_ge(s_po, NG * b + g + 1)
                o = po[:, 0:TT * HG * (HD + 1)].rearrange("p (n d) -> p n d", d=HD + 1)
                ch.link(V.reciprocal(o_rec[:], o[:, :, HD]))
                last_op = V.tensor_tensor(o_tok[:].rearrange("p c (h d) -> p (c h) d", h=HG), o[:, :, 0:HD],
                                          o_rec[:].unsqueeze(2).to_broadcast([P, TT * HG, HD]), ALU.mult)
                last_op.then_inc(s_norm, 1)

            def ln_stats(ch, n, buf):
                for c in range(TT):
                    i = V.bn_stats(stats[:, n, c, :], buf[:, c, :])
                ch.link(i)
                V.memset(spare[:, n:n + 1], 0.0)
                for c in range(TT):
                    i = V.bn_aggr(meanvar[:, n, c, :], stats[:, n, c, :])
                i.then_inc(ln_stat[n], 1)

            def ln_apply(n, b, src, dst, ready):
                dve.wait_ge(ln_rstd[n], b + 1)
                for c in range(TT):
                    i = V.tensor_scalar(dst[:, c, :], src[:, c, :], meanvar[:, n, c, 0:1], rstd[:, n, c:c + 1],
                                        ALU.subtract, ALU.mult)
                i.then_inc(ready, 1)

            def recurrence_start(ch, b, c):
                i, k = c % HC, pw[:, S * (c % HC):S * (c % HC + 1)]
                dve.wait_ge(w_job, W_JOBS * b + W_X1J + c // HC + 1)
                if c >= HC:
                    dve.wait_ge(w_den, 2 * (CC * b + c - HC + 1))
                V.tensor_tensor_scan(w_max[:, i, 1:S + 1], decay[:, c:c + 1].to_broadcast([P, S]), k,
                                     START_MAX, ALU.add, ALU.max).then_inc(w_pp, 1)
                dve.wait_ge(w_pp, CC * b + c + 1)
                ch.mark(V.scalar_tensor_tensor(w_d[:, i, :], k, first[:, c:c + 1], w_max[:, i, 0:S],
                                               ALU.add, ALU.subtract))
                e2 = V.tensor_tensor(w_e2[:, i, 1:S + 1], k, w_max[:, i, 1:S + 1], ALU.subtract)
                e2.then_inc(w_free if i == HC - 1 else w_even, 1)

            def recurrence_clamp(ch, b, c):
                i = c % HC
                if c >= HC:
                    dve.wait_ge(w_yr, CC * b + c - HC + 1)
                ch.wait()
                ch.link(V.tensor_scalar(w_key[:, i, :], w_d[:, i, :], -1.0, 0.0, ALU.mult, ALU.min))
                V.tensor_scalar(w_d[:, i, :], w_d[:, i, :], 0.0, None, ALU.min).then_inc(w_min, 1)

            def sums(b, c):
                i = c % HC
                dve.wait_ge(w_carry, CC * b + c + 1)
                dve.wait_ge(w_evr, CC * b + c + 1)
                V.tensor_tensor_scan(w_e2[:, i, 1:S + 1], w_e1[:, i, :], w_e2[:, i, 1:S + 1], 0.0,
                                     ALU.mult, ALU.add)
                V.tensor_tensor_scan(w_max[:, i, 1:S + 1], w_e1[:, i, :], w_ev[:, i, :], 0.0,
                                     ALU.mult, ALU.add).then_inc(w_scan, 1)

            def divide(b, c):
                dve.wait_ge(w_den, 2 * (CC * b + c) + 1)
                V.reciprocal(w_key[:, c % HC, :], w_key[:, c % HC, :]).then_inc(w_rec, 1)

            def second_residual(b, half):
                dve.wait_ge(w_job, W_JOBS * b + W_YJ + half + 1)
                cols = slice(HC * P * half, HC * P * (half + 1))
                V.tensor_tensor(xa[:, :, cols], pw[:].rearrange("p (c d) -> p c d", c=TT), xa[:, :, cols],
                                ALU.add).then_inc(w_free, 1)

            def second_stats(ch, b):
                dve.wait_ge(w_free, W_JOBS * b + W_YJ + 2)
                ln_stats(ch, 1, xa)

            def second_norm(b):
                wait(dve, stored, 16 * b)
                ln_apply(1, b, xa, xb, x2_ready)

            def x2_split_lo(b, half):
                dve.wait_ge(x2_hi, 2 * b + half + 1)
                part = slice(HC * half, HC * (half + 1))
                bank, s_free = ((pw, w_free), (pp, pf_free))[half]
                V.tensor_tensor(xt_lo[:, part, :].rearrange("p c t -> p (c t)"), bank[:],
                                xt_hi[:, part, :].rearrange("p c t -> p (c t)").bitcast(f32), ALU.subtract)\
                    .then_inc(s_free, 1)

            def qk_lo(b, job):
                which, n = (0, job - PA_Q) if job < PA_K else (1, job - PA_K)
                hi, lo = (q_hi, k_hi)[which], (q_lo, k_lo)[which]
                dve.wait_ge(pa_hi, 4 * b + job + 1)
                for i in range(2):
                    c = 2 * n + i
                    o = V.scalar_tensor_tensor(lo[:, c, :], pp[:, S * i:S * (i + 1)], ch_bias[:, which, c:c + 1],
                                               hi[:, c, :].bitcast(f32), ALU.add, ALU.subtract)
                o.then_inc(pa_free, 1)

            def fq_lo(b, n):
                dve.wait_ge(pf_hi, 2 * b + n + 1)
                V.tensor_tensor(q_lo[:, 2 * n:2 * n + 2, :].rearrange("p c t -> p (c t)"), pp[:],
                                q_hi[:, 2 * n:2 * n + 2, :].rearrange("p c t -> p (c t)").bitcast(f32),
                                ALU.subtract).then_inc(pf_free, 1)

            def out_lo(b, g):
                dve.wait_ge(ot_hi, NG * b + g + 1)
                V.scalar_tensor_tensor(k_lo[:, g, :], pt[:, 0:S], ch_bias[:, 2, g:g + 1],
                                       k_hi[:, g, :].bitcast(f32), ALU.add, ALU.subtract).then_inc(a_free, 1)

            def normalise_a(ch, b, g):
                if g:
                    dve.wait_ge(a_job, A_JOBS * b + A_OT[g - 1] + 1)
                normalise(ch, b, g, a_po, a_norm)

            def first_residual(b, c):
                if c == 0:
                    dve.wait_ge(xa_ready, b + 1)
                dve.wait_ge(pa_job, PA_JOBS * b + PA_WO + c + 1)
                V.tensor_tensor(xa[:, c, :], pp[:], xa[:, c, :], ALU.add).then_inc(pa_free, 1)

            def first_stats(ch, b):
                dve.wait_ge(pa_free, PA_JOBS * (b + 1))
                ln_stats(ch, 0, xa)

            def gate_out(b):
                dve.wait_ge(w_job, W_JOBS * b + W_GATE + 1)
                V.tensor_copy(logit_t[0:NH, :], pw[0:NH, 0:S]).then_inc(w_free, 1)

            def gating(ch, b):
                dve.wait_ge(w_job, W_JOBS * b + W_GATE_T + 1)
                V.tensor_copy(logit[:], pw[:, 0:TT * P].rearrange("p (c h) -> p c h", c=TT)[:, :, 0:NH]).then_inc(w_free, 1)
                dve.wait_ge(w_free, W_JOBS * (b + 1))
                ch.mark(V.tensor_reduce(g_max[:], logit[:], AX.X, ALU.max))
                V.tensor_reduce(g_nmax[:], logit[:], AX.X, ALU.max, negate=True).then_inc(g_ready, 1)
                ch.wait()
                ch.link(V.tensor_tensor(g_eq[:], logit[:], g_max[:].unsqueeze(2).to_broadcast([P, TT, NH]),
                                        ALU.is_equal))
                ch.link(V.tensor_tensor(g_rank[:], g_eq[:], rank[:].unsqueeze(1).to_broadcast([P, TT, NH]),
                                        ALU.mult))
                ch.link(V.tensor_reduce(g_top[:], g_rank[:], AX.X, ALU.max))
                ch.link(V.tensor_tensor(g_ind[:], g_rank[:], g_top[:].unsqueeze(2).to_broadcast([P, TT, NH]),
                                        ALU.is_equal))
                dve.wait_ge(g_summed, b + 1)
                ch.link(V.reciprocal(g_val[:], g_sum[:]))

            def pick(ch, b, job, c, dst):
                dve.wait_ge(pf_job, PF_JOBS * b + job + c + 1)
                V.tensor_tensor(picked, pp[:].rearrange("p (h d) -> p h d", h=NH),
                                g_ind[:, c, :].unsqueeze(2).to_broadcast([P, NH, HD]), ALU.mult).then_inc(pf_free, 1)
                dve.wait_ge(pf_free, PF_JOBS * b + job + c + 1)
                ch.link(V.tensor_reduce(dst[:, c, :], picked.rearrange("p h d -> p d h"), AX.X, ALU.add))

            def pick_key(ch, b, c):
                pick(ch, b, PF_K, c, k_sel)
                ch.link(V.tensor_copy(k3[:, c, 0:3:2, :], k_sel[:, c, :].unsqueeze(1).to_broadcast([P, 2, HD])))
                ch.link(V.tensor_tensor(k3[:, c, 1, :], k_sel[:, c, :], k3[:, c, 0, :].bitcast(f32), ALU.subtract))

            def pick_value(ch, b, c):
                pick(ch, b, PF_V, c, v_sel)
                ch.link(V.tensor_scalar(v_f[:, c, 0:HD], v_sel[:, c, :], g_val[:, c:c + 1], None, ALU.mult))

            def third_residual(ch, b, g):
                normalise(ch, b, g, f_po, f_norm)
                dve.wait_ge(f_norm, NG * b + g + 1)
                cols = slice(P * g, P * (g + 1))
                ch.link(V.tensor_tensor(xb[:, :, cols], xb[:, :, cols], o_tok[:], ALU.add))

            def iteration(t, do_a, prev, nxt):
                b = t - 1
                if do_a:
                    cha, chw = Chain(dve, dve_a, A_LINKS, t), Chain(dve, dve_w, W_LINKS, t)
                    cha.n = 1
                if prev:
                    chf, chy = Chain(dve, dve_f, F_LINKS, b), Chain(dve, dve_w, W_LINKS, b)
                    chy.n = W_LINKS - 1
                if nxt:
                    chn = Chain(dve, dve_a, A_LINKS, t + 1)
                if do_a:
                    maxima_a(cha, t, 1, 0, 1)
                if prev:
                    divide(b, 3)
                if do_a:
                    maxima_a(cha, t, 1, 2)
                    rows_a(t, 1)
                if prev and not (isinstance(t, int) and t < 2):
                    ln_apply(2, t - 2, xb, xb, x3_ready)
                if do_a:
                    normalise_a(cha, t, 0)
                    if not prev:
                        split_lo(W_O)
                if prev:
                    second_residual(b, 1)
                    second_stats(chy, b)
                    chy.close()
                if do_a:
                    maxima_a(cha, t, 2, 0, 1)
                if prev:
                    second_norm(b)
                if do_a:
                    out_lo(t, 0)
                    maxima_a(cha, t, 2, 2)
                if prev:
                    x2_split_lo(b, 0)
                    x2_split_lo(b, 1)
                if do_a:
                    rows_a(t, 2)
                    normalise_a(cha, t, 1)
                    if not prev:
                        split_lo(W_FQ)
                if prev:
                    fq_lo(b, 0)
                if do_a:
                    maxima_a(cha, t, 3, 0, 1)
                    out_lo(t, 1)
                if prev:
                    fq_lo(b, 1)
                if do_a:
                    maxima_a(cha, t, 3, 2)
                if prev:
                    gate_out(b)
                    gating(chf, b)
                if do_a:
                    rows_a(t, 3)
                if prev:
                    pick_key(chf, b, 0)
                if do_a:
                    normalise_a(cha, t, 2)
                    if not prev:
                        split_lo(W_FK)
                if prev:
                    pick_key(chf, b, 1)
                if do_a:
                    out_lo(t, 2)
                if prev:
                    dve.wait_ge(f_job, F_JOBS * b + F_KT + 1)
                    V.tensor_copy(kf_stack[0:3 * HD, :], pt[0:3 * HD, 0:S]).then_inc(f_free, 1)
                    assert chf.n == F_LINK_K3
                    maxima_f(chf, b, 0)
                    pick_value(chf, b, 0)
                    rows_f(b, 0, a_mrow[NG - 1], 16 * (t + 1 if do_a else NB))
                if do_a:
                    normalise_a(cha, t, 3)
                    if not prev:
                        split_lo(W_FV)
                if prev:
                    pick_value(chf, b, 1)
                    assert chf.n == F_LINK_PICKED + 1
                    maxima_f(chf, b, 1)
                if do_a:
                    out_lo(t, 3)
                if prev:
                    rows_f(b, 1)
                    third_residual(chf, b, 0)
                if do_a:
                    first_residual(t, 0)
                    first_residual(t, 1)
                    first_stats(cha, t)
                    cha.close()
                if prev:
                    maxima_f(chf, b, 2, 0, 1)
                if do_a:
                    ln_apply(0, t, xa, xa, x1_ready)
                if prev:
                    maxima_f(chf, b, 2, 2)
                if nxt:
                    qk_lo(t + 1, PA_Q)
                if do_a:
                    recurrence_start(chw, t, 0)
                    recurrence_clamp(chw, t, 0)
                if prev:
                    rows_f(b, 2)
                if do_a:
                    recurrence_start(chw, t, 1)
                    recurrence_clamp(chw, t, 1)
                if prev:
                    third_residual(chf, b, 1)
                if nxt:
                    qk_lo(t + 1, PA_Q + 1)
                if prev:
                    maxima_f(chf, b, 3, 0, 1)
                if do_a:
                    sums(t, 0)
                    sums(t, 1)
                if nxt:
                    qk_lo(t + 1, PA_K)
                if prev:
                    maxima_f(chf, b, 3, 2)
                if prev:
                    rows_f(b, 3)
                if do_a:
                    divide(t, 0)
                    recurrence_start(chw, t, 2)
                if prev:
                    third_residual(chf, b, 2)
                if nxt:
                    qk_lo(t + 1, PA_K + 1)
                if do_a:
                    divide(t, 1)
                    recurrence_clamp(chw, t, 2)
                    recurrence_start(chw, t, 3)
                    recurrence_clamp(chw, t, 3)
                if nxt:
                    maxima_a(chn, t + 1, 0)
                if do_a:
                    sums(t, 2)
                    second_residual(t, 0)
                if nxt:
                    if prev:
                        rows_a(t + 1, 0, f_mrow[NG - 1], 16 * t)
                    else:
                        rows_a(t + 1, 0, a_mrow[NG - 1], 16 * (t + 1))
                if do_a:
                    sums(t, 3)
                if prev:
                    third_residual(chf, b, 3)
                    ln_stats(chf, 2, xb)
                    chf.close()
                if do_a:
                    divide(t, 2)

            V.memset(v_a[:, :, :, HD:HD + 1], 1.0)
            V.memset(v_f[:, :, HD:HD + 1], 1.0)
            V.memset(logit_t[:], 0.0).then_inc(dve_once, 1)
            V.memset(k_stack[3 * HD:3 * HD + 2, 0:NH - HG, :].bitcast(f32), 1.0)
            V.memset(w_max[:, :, 0:1], START_MAX)
            V.memset(w_e2[:, :, 0:1], 0.0)
            V.memset(eps[:], EPS)
            dve.wait_ge(dve_once, 1)
            V.memset(kf_stack[3 * HD:3 * HD + 2, :].bitcast(f32), 1.0)
            dve.wait_ge(w_split_hi, 1)
            V.tensor_tensor(gate_lo[:], gate, gate_hi[:].bitcast(f32), ALU.subtract)
            V.memset(minus_half[:], -0.5).then_inc(consts, 1)
            split_lo(W_Q, W_K)
            dve.wait_ge(consts, CONSTS)
            dve.wait_ge(act_once, 2)

            for job in range(PA_V):
                qk_lo(0, job)
            split_lo(W_V)
            maxima_a(Chain(dve, dve_a, A_LINKS, 0), 0, 0)
            rows_a(0, 0)
            iteration(0, True, False, True)
            iteration(1, True, True, True)
            with dve.Fori(2, NB - 1) as t:
                iteration(t, True, True, True)
            iteration(NB - 1, True, True, False)
            iteration(NB, False, True, False)
            ln_apply(2, NB - 1, xb, xb, x3_ready)

        @block.gpsimd
        def _(pool):
            def inverse_std(b, n):
                pool.wait_ge(ln_stat[n], b + 1)
                G.tensor_tensor(var_eps[:, n, :], meanvar[:, n, :, 1], eps[:], ALU.add).then_inc(pool_ln[n], 1)
                pool.wait_ge(pool_ln[n], b + 1)
                G.tensor_tensor(rstd[:, n, :], var_eps[:, n, :], minus_half[:], ALU.pow).then_inc(ln_rstd[n], 1)

            def add_bo(b):
                pool.wait_ge(load_xa, 16 * (b + 1))
                for c in range(TT):
                    i = G.tensor_tensor(xa[:, c, :], xa[:, c, :], bo_row[:], ALU.add)
                i.then_inc(xa_ready, 1)

            def x_split_lo(b):
                pool.wait_ge(xt_hi_ready, b + 1)
                G.tensor_tensor(xt_lo[:], x_raw[:], xt_hi[:].bitcast(f32), ALU.subtract).then_inc(xt_ready, 1)

            now, after = slice(1, S + 1), slice(0, S)

            def difference(b, c):
                pool.wait_ge(w_pp, CC * b + c + 1)
                G.tensor_tensor(w_e1[:, c % HC, :], w_max[:, c % HC, after], w_max[:, c % HC, now],
                                ALU.subtract).then_inc(w_diff, 1)

            def weighted(b, c):
                i = c % HC
                pool.wait_ge(w_carry, CC * b + c + 1)
                pool.wait_ge(load_v[i], 16 * (HC * b + c // HC + 1))
                G.tensor_tensor(w_ev[:, i, :], w_e2[:, i, now], w_val[:, i, :], ALU.mult).then_inc(w_evr, 1)

            def products(b, c):
                i = c % HC
                ch = Chain(pool, pool_w, 3 * CC, b)
                ch.n = 3 * c
                pool.wait_ge(w_scan, CC * b + c + 1)
                pool.wait_ge(w_now, CC * b + c + 1)
                ch.mark(G.tensor_tensor(w_e1[:, i, :], w_key[:, i, :], w_max[:, i, after], ALU.mult))
                ch.mark(G.tensor_tensor(w_ev[:, i, :], w_d[:, i, :], w_val[:, i, :], ALU.mult))
                ch.mark(G.tensor_tensor(w_key[:, i, :], w_key[:, i, :], w_e2[:, i, after], ALU.mult))
                ch.wait()
                G.tensor_tensor(w_key[:, i, :], w_key[:, i, :], w_d[:, i, :], ALU.add).then_inc(w_den, 1)
                G.tensor_tensor(w_ev[:, i, :], w_e1[:, i, :], w_ev[:, i, :], ALU.add).then_inc(w_den, 1)

            def quotient(b, c):
                i = c % HC
                pool.wait_ge(w_den, 2 * (CC * b + c + 1))
                pool.wait_ge(w_rec, CC * b + c + 1)
                wait(pool, w_job, W_JOBS * (b - 1) + W_YJ + 2 if c < HC else W_JOBS * b + W_YJ + 1)
                G.tensor_tensor(w_y[:, i, :], w_ev[:, i, :], w_key[:, i, :], ALU.mult).then_inc(w_yr, 1)

            def ones_back(b):
                pool.wait_ge(w_yr, CC * (b + 1))
                G.tensor_tensor(spare_pool[0:1, :], eps[0:1, 0:1], eps[0:1, 0:1], ALU.add)
                G.memset(k_stack[3 * HD:3 * HD + 2, NH - HG:, :].bitcast(f32), 1.0).then_inc(w_ones, 1)
                pool.wait_ge(w_ones, b + 2)

            G.memset(ident[:], 0.0).then_inc(zero_done, 1)
            G.memset(mask_qk[:], 0.0).then_inc(zero_done, 1)
            G.memset(mask_kq[:], 0.0).then_inc(zero_done, 1)
            G.iota(rank[:], pattern=[[-1, NH]], base=NH, channel_multiplier=0,
                   allow_small_or_imprecise_dtypes=True).then_inc(zero_done, 1)
            pool.wait_ge(zero_done, 4)
            G.affine_select(out=ident[:], in_=ident[:], compare_op=ALU.not_equal, fill=1.0, base=0,
                            pattern=[[-1, P]], channel_multiplier=1).then_inc(pool_once, 1)
            G.affine_select(out=mask_qk[:], in_=mask_qk[:], compare_op=ALU.is_ge, fill=MASKED, base=0,
                            pattern=[[-1, P]], channel_multiplier=1).then_inc(pool_once, 1)
            G.affine_select(out=mask_kq[:], in_=mask_kq[:], compare_op=ALU.is_ge, fill=MASKED, base=0,
                            pattern=[[1, P]], channel_multiplier=-1).then_inc(pool_once, 1)
            pool.wait_ge(pool_once, 3)
            G.tensor_copy(ident_b[:], ident[:]).then_inc(consts, 1)
            pool.wait_ge(consts, CONSTS)
            G.memset(k_stack[3 * HD:3 * HD + 2, NH - HG:, :].bitcast(f32), 1.0).then_inc(w_ones, 1)
            pool.wait_ge(w_ones, 1)
            x_split_lo(0)

            def iteration(t, prev, nxt):
                if prev:
                    inverse_std(t - 1, 1)
                add_bo(t)
                if nxt:
                    x_split_lo(t + 1)
                inverse_std(t, 0)
                difference(t, 0)
                difference(t, 1)
                weighted(t, 0)
                weighted(t, 1)
                products(t, 0)
                products(t, 1)
                quotient(t, 0)
                difference(t, 2)
                quotient(t, 1)
                difference(t, 3)
                weighted(t, 2)
                weighted(t, 3)
                products(t, 2)
                if prev:
                    inverse_std(t - 1, 2)
                products(t, 3)
                quotient(t, 2)
                quotient(t, 3)
                ones_back(t)

            iteration(0, False, True)
            iteration(1, True, True)
            with pool.Fori(2, NB - 1) as t:
                iteration(t, True, True)
            iteration(NB - 1, True, False)
            inverse_std(NB - 1, 1)
            inverse_std(NB - 1, 2)


def kernel(**inputs):
    import numpy as np
    import concourse.bacc as bacc
    from concourse.bass_utils import run_bass_kernel_spmd as run

    a = {n: np.asarray(v) for n, v in inputs.items()}

    def quadrants(w):
        return w.reshape(NG, CC, HD, -1).transpose(1, 0, 2, 3).reshape(D, -1)

    wqkv = a["L0_ffn_W_qkv"]
    mats = [quadrants(a["L0_attn_Wq"]), quadrants(a["L0_attn_Wk"]), a["L0_attn_Wv"], a["L0_attn_Wo"],
            quadrants(wqkv[0:D]), wqkv[D:2 * D], wqkv[2 * D:3 * D]]
    arrays = {
        "x": a["x"],
        "xT": a["x"].transpose(0, 2, 1),
        "ctxT": a["ctx_2048"].transpose(0, 2, 1),
        "weights": np.stack([m.T.reshape(CC, P, D) for m in mats]),
        "gate": a["L0_ffn_W_gate"].T,
        "ch_bias": np.stack([quadrants(a["L0_attn_bq"].reshape(D, 1)).reshape(CC, P).T,
                             quadrants(a["L0_attn_bk"].reshape(D, 1)).reshape(CC, P).T,
                             a["L0_attn_bv"].reshape(CC, P).T], axis=1),
        "row_bias": np.broadcast_to(a["L0_attn_bo"], (P, D)),
        "decay": a["L0_xattn_time_decay"].reshape(CC, P).T,
        "first": a["L0_xattn_time_first"].reshape(CC, P).T,
    }
    nc = bacc.Bacc("TRN2", target_bir_lowering=False, num_devices=1)
    fed, args = {}, []
    for name, v in arrays.items():
        v = np.ascontiguousarray(v)
        fed[f"in_{name}"] = v
        args.append(nc.dram_tensor(f"in_{name}", v.shape, mybir.dt.from_np(v.dtype), kind="ExternalInput").ap())
    out = nc.dram_tensor("out_y", (NB, S, D), mybir.dt.float32, kind="ExternalOutput").ap()
    build(nc, *args, out)
    return run(nc, [fed], core_ids=[0]).results[0]["out_y"]
```
